# Optimizing a Trainium2 kernel written in Bass

```python
import numpy as np
import jax
import jax.numpy as jnp

def _softmax(x, axis=-1):
    return jax.nn.softmax(x, axis=axis)

def _gelu(x):
    return jax.nn.gelu(x, approximate=True)

def _silu(x):
    return jax.nn.silu(x)

def _sigmoid(x):
    return jax.nn.sigmoid(x)

def _layernorm(x, axis=-1, eps=1e-05):
    m = jnp.mean(x, axis=axis, keepdims=True)
    v = jnp.var(x, axis=axis, keepdims=True)
    return (x - m) / jnp.sqrt(v + eps)

def _scatter_add(tgt, idx, src, axis=0):
    return tgt.at[idx].add(src)

def _segment_sum(src, seg, n):
    return jax.ops.segment_sum(src, seg, n)
kernel_name = 'mk_xattn_ffn_d1_seqx_r2_9add9e'

def setup_inputs(seed: int=0):
    np.random.seed(seed)
    _w = jnp.asarray

    def _rec_inputs():
        import jax
        import jax.numpy as jnp
        _rk = jax.random.key(seed)
        x = 0.000341 + 1 * jax.random.normal(jax.random.fold_in(_rk, 1), (8, 512, 1024), jnp.float32)
        _lenS = 512 - jax.random.randint(jax.random.fold_in(_rk, 7), (8,), 0, max(1, 512 // 4) + 1, jnp.int32)
        _lenS2 = 512 - jax.random.randint(jax.random.fold_in(_rk, 8), (8,), 0, max(1, 512 // 4) + 1, jnp.int32)
        _ctx_2048P = jax.random.normal(jax.random.fold_in(_rk, 11), (8, 16, 1024), jnp.float32)
        _ctx_2048c = jax.random.dirichlet(jax.random.fold_in(_rk, 511), 0.3 * jnp.ones((16,), jnp.float32), (8, 512))
        _ctx_2048t = jnp.einsum('bsk,bkd->bsd', _ctx_2048c, _ctx_2048P)
        _ctx_2048t = _ctx_2048t * jax.lax.rsqrt(jnp.mean(jnp.square(_ctx_2048t)) + 1e-12) * 0.953939
        ctx_2048 = -1.47943e-05 + 1.00017 * (_ctx_2048t + 0.3 * jax.random.normal(jax.random.fold_in(_rk, 611), (8, 512, 1024), jnp.float32))
        return (x, ctx_2048)
    x, ctx_2048 = _rec_inputs()

    def _L0_xattn_setup():
        import jax, jax.numpy as jnp
        import numpy as np

        def _wkv(time_decay, time_first, k, v):
            w = -jnp.exp(time_decay)
            u = time_first
            B, T, C = k.shape
            aa = jnp.zeros((B, C), dtype=k.dtype)
            bb = jnp.zeros((B, C), dtype=k.dtype)
            pp = jnp.full((B, C), -1e+38, dtype=k.dtype)

            def step(carry, kv_t):
                aa, bb, pp = carry
                kt, vt = kv_t
                ww = u + kt
                q = jnp.maximum(pp, ww)
                e1 = jnp.exp(pp - q)
                e2 = jnp.exp(ww - q)
                y_t = (e1 * aa + e2 * vt) / (e1 * bb + e2)
                ww2 = pp + w
                q2 = jnp.maximum(ww2, kt)
                e1b = jnp.exp(ww2 - q2)
                e2b = jnp.exp(kt - q2)
                new_carry = (e1b * aa + e2b * vt, e1b * bb + e2b, q2)
                return (new_carry, y_t)
            ks = jnp.transpose(k, (1, 0, 2))
            vs = jnp.transpose(v, (1, 0, 2))
            _, ys = jax.lax.scan(step, (aa, bb, pp), (ks, vs))
            return jnp.transpose(ys, (1, 0, 2))
        key = jax.random.key(seed)
        k1, k2, k3, k4 = jax.random.split(key, 4)
        B, T, C = (8, 512, 1024)
        return {'batch_size': B, 'seq_len': T, 'embedding_dim': C, 'time_decay': jax.random.normal(k1, (C,), dtype=jnp.float32), 'time_first': jax.random.normal(k2, (C,), dtype=jnp.float32), 'k': jax.random.normal(k3, (B, T, C), dtype=jnp.float32), 'v': jax.random.normal(k4, (B, T, C), dtype=jnp.float32)}
    _L0_xattn_all = _L0_xattn_setup()
    _L0_xattn_in = {k: v for k, v in _L0_xattn_all.items() if k in ('time_decay', 'time_first')}
    del _L0_xattn_all

    def _L0_ffn_setup():
        import jax, jax.numpy as jnp
        import numpy as np
        B, T, D, E, H = (4, 1024, 1024, 4, 4096)
        TOPK = 2
        CAPACITY_FACTOR = 1
        key = jax.random.key(seed)
        k0, k1, k2, k3 = jax.random.split(key, 4)
        x = jax.random.normal(k0, (B, T, D), dtype=jnp.float32)
        Wg = jax.random.normal(k1, (D, E), dtype=jnp.float32) * 0.02
        bg = jnp.zeros((E,), dtype=jnp.float32)
        W1 = jax.random.normal(k2, (E, D, H), dtype=jnp.float32) * (1.0 / np.sqrt(D))
        W2 = jax.random.normal(k3, (E, H, D), dtype=jnp.float32) * (1.0 / np.sqrt(H))
        return {'x': x, 'Wg': Wg, 'bg': bg, 'W1': W1, 'W2': W2}
    _L0_ffn_all = _L0_ffn_setup()
    _L0_ffn_in = {k: v for k, v in _L0_ffn_all.items() if k in ('Wg', 'bg', 'W1', 'W2')}
    del _L0_ffn_all
    return {'x': x, 'ctx_2048': ctx_2048, 'L0_xattn_time_decay': _L0_xattn_in['time_decay'], 'L0_xattn_time_first': _L0_xattn_in['time_first'], 'L0_ffn_Wg': _L0_ffn_in['Wg'], 'L0_ffn_bg': _L0_ffn_in['bg'], 'L0_ffn_W1': _L0_ffn_in['W1'], 'L0_ffn_W2': _L0_ffn_in['W2']}

def reference(x, ctx_2048, L0_xattn_time_decay, L0_xattn_time_first, L0_ffn_Wg, L0_ffn_bg, L0_ffn_W1, L0_ffn_W2):
    import jax
    import jax.numpy as jnp

    def _L0_xattn_ref(batch_size, seq_len, embedding_dim, time_decay, time_first, k, v):
        import jax, jax.numpy as jnp
        import numpy as np

        def _wkv(time_decay, time_first, k, v):
            w = -jnp.exp(time_decay)
            u = time_first
            B, T, C = k.shape
            aa = jnp.zeros((B, C), dtype=k.dtype)
            bb = jnp.zeros((B, C), dtype=k.dtype)
            pp = jnp.full((B, C), -1e+38, dtype=k.dtype)

            def step(carry, kv_t):
                aa, bb, pp = carry
                kt, vt = kv_t
                ww = u + kt
                q = jnp.maximum(pp, ww)
                e1 = jnp.exp(pp - q)
                e2 = jnp.exp(ww - q)
                y_t = (e1 * aa + e2 * vt) / (e1 * bb + e2)
                ww2 = pp + w
                q2 = jnp.maximum(ww2, kt)
                e1b = jnp.exp(ww2 - q2)
                e2b = jnp.exp(kt - q2)
                new_carry = (e1b * aa + e2b * vt, e1b * bb + e2b, q2)
                return (new_carry, y_t)
            ks = jnp.transpose(k, (1, 0, 2))
            vs = jnp.transpose(v, (1, 0, 2))
            _, ys = jax.lax.scan(step, (aa, bb, pp), (ks, vs))
            return jnp.transpose(ys, (1, 0, 2))
        assert seq_len <= 512
        return _wkv(time_decay, time_first, k, v)

    def _L0_ffn_ref(x, Wg, bg, W1, W2):
        import jax, jax.numpy as jnp
        import numpy as np
        B, T, D, E, H = (4, 1024, 1024, 4, 4096)
        TOPK = 2
        CAPACITY_FACTOR = 1
        Bq, Tq, Dq = x.shape
        N = Bq * Tq
        capacity = int(N * CAPACITY_FACTOR / E)
        flat_x = x.reshape(N, Dq)
        logits = flat_x @ Wg + bg
        top_vals, top_idx = jax.lax.top_k(logits, TOPK)
        sparse = jnp.full_like(logits, -jnp.inf)
        sparse = sparse.at[jnp.arange(N)[:, None], top_idx].set(top_vals)
        probs = jax.nn.softmax(sparse, axis=-1)
        out = jnp.zeros_like(flat_x)
        for i in range(E):
            assigned = (top_idx == i).any(axis=-1)
            score = jnp.where(assigned, probs[:, i], -jnp.inf)
            sel_p, sel_idx = jax.lax.top_k(score, capacity)
            p = jnp.where(jnp.isfinite(sel_p), sel_p, 0.0)[:, None]
            tok = flat_x[sel_idx]
            h = jax.nn.gelu(tok @ W1[i], approximate=False)
            y = h @ W2[i] * p
            out = out.at[sel_idx].add(y)
        return out.reshape(Bq, Tq, Dq)
    x = x + _L0_xattn_ref(8, 512, 1024, L0_xattn_time_decay, L0_xattn_time_first, _layernorm(x, axis=-1), ctx_2048)
    x = x + _L0_ffn_ref(_layernorm(x, axis=-1), L0_ffn_Wg, L0_ffn_bg, L0_ffn_W1, L0_ffn_W2)
    return x

_drawn_inputs = setup_inputs


def setup_inputs(seed=0):
    import zlib

    import numpy as np

    out = dict(_drawn_inputs(seed))
    spreads = {'L0_ffn_bg': (0.0, 0.1)}
    factors = {}
    for name, (base, spread) in spreads.items():
        noise = np.random.default_rng([zlib.crc32(name.encode()), seed]).standard_normal(out[name].shape)
        drawn = base * np.exp(spread * noise) if base else spread * noise
        out[name] = jnp.asarray(drawn.astype(out[name].dtype))
    for name, factor in factors.items():
        out[name] = (out[name] * factor).astype(out[name].dtype)
    return out
```

```python
from contextlib import ExitStack

import concourse.bass as bass
from concourse import mybir

P = 128
F32 = mybir.dt.float32
F32R = mybir.dt.float32r
BF16 = mybir.dt.bfloat16
U32 = mybir.dt.uint32
ALU = mybir.AluOpType
ACT = mybir.ActivationFunctionType
AX_X = mybir.AxisListType.X

LN_EPS = 1e-5
EXP_LN_TABLE = 6
TOPK = 2


def at_least(engine, semaphore, value):
    if isinstance(value, int) and value <= 0:
        return
    engine.wait_ge(semaphore, value)


def token_mixing(nc, x, v, time_decay, time_first, w_gate, b_gate, out, z_dram, logits, ident):
    B, T, C = x.shape
    TT = T // P
    CC = C // P
    E = w_gate.shape[1]
    HALF = 512
    PAIRS = CC // 2

    x_dram = x.rearrange("b (t p) c -> b p t c", p=P)
    v_dram = v.rearrange("b (t p) c -> b p t c", p=P)
    out_dram = out.rearrange("b (t p) c -> b p t c", p=P)
    z_out_dram = z_dram.rearrange("(b t p) c -> b p t c", p=P, t=TT)

    with ExitStack() as ctx:
        def sb(name, shape, dt=F32):
            return ctx.enter_context(nc.sbuf_tensor(name, shape, dt))

        def ps(name, shape, dt=F32):
            return ctx.enter_context(nc.psum_tensor(name, shape, dt))

        def sem(name):
            return ctx.enter_context(nc.semaphore(name))

        x_sb = sb("x_sb", [P, 2, TT, C])
        v_sb = sb("v_sb", [P, 2, TT, C])
        ek = sb("ek", [P, 2, TT, C])
        x1_sb = sb("x1_sb", [P, TT, C])
        state = sb("state", [P, 2, 2, T + 1])
        now = sb("now", [P, 4, 2, T])
        dn = sb("dn", [P, 4, 2, T])
        recip = sb("recip", [P, 2, 2, T])
        neg_y = sb("neg_y", [P, CC, T])
        z_sb = sb("z_sb", [P, TT, C])
        z_t = sb("z_t", [P, 2, CC, P])
        wg_sb = sb("wg_sb", [P, CC, E])
        bg_sb = sb("bg_sb", [P, E])
        td_sb = sb("td_sb", [P, CC])
        tf_sb = sb("tf_sb", [P, CC])
        decay = sb("decay", [P, CC])
        scale_a = sb("scale_a", [P, CC])
        scale_b = sb("scale_b", [P, CC])
        eps = sb("eps", [P, 1])
        bn = sb("bn", [P, 2, TT, 2, 6])
        mv = sb("mv", [P, 2, TT, 2])
        ln_tmp = sb("ln_tmp", [P, 2, 8, TT])
        rstd = sb("rstd", [P, 2, TT])
        shift = sb("shift", [P, 2, TT])

        ps_dn = ps("ps_dn", [P, 2, 2, T])
        ps_y = ps("ps_y", [P, 2, HALF])
        ps_z = ps("ps_z", [P, HALF])
        ps_lg = ps("ps_lg", [P, HALF])

        x_in = [[sem(f"x_in{par}_{t}") for t in range(TT)] for par in range(2)]
        v_in = [sem("v_in0"), sem("v_in1")]
        x1_out = sem("x1_out")
        z_out = sem("z_out")
        par_in = sem("par_in")
        eps_set = sem("eps_set")
        clipped = sem("clipped")
        dec_exp = sem("dec_exp")
        params_ready = sem("params_ready")
        ident_zero = sem("ident_zero")
        ident_ready = sem("ident_ready")
        bn_done = sem("bn_done")
        mv_ready = [sem("mv1_ready"), sem("mv2_ready")]
        log_done = sem("log_done")
        seed_ready = [sem("seed1_ready"), sem("seed2_ready")]
        refine = sem("refine")
        ln_ready = [sem("ln1_ready"), sem("ln2_ready")]
        ek_ready = sem("ek_ready")
        ekv_ready = sem("ekv_ready")
        dn_t_ready = sem("dn_t_ready")
        now_ready = sem("now_ready")
        scan_done = sem("scan_done")
        dn_ready = sem("dn_ready")
        ln_den = sem("ln_den")
        recip_ready = sem("recip_ready")
        quot_ready = sem("quot_ready")
        y_ready = sem("y_ready")
        yt_ready = sem("yt_ready")
        x1_ready = sem("x1_ready")
        z_ready = sem("z_ready")
        zt_ready = sem("zt_ready")
        zt_copied = sem("zt_copied")
        lg_done = sem("lg_done")
        logits_out = sem("logits_out")
        waited_sp, waited_dve = sem("waited_sp"), sem("waited_dve")

        def loads(b, par):
            return b + (2 if par == 0 else 1)

        def before_start(b, back):
            return isinstance(b, int) and b < back

        def is_last(b):
            return isinstance(b, int) and b == B - 1

        def over_batches(engine, body):
            body(0, 0)
            body(1, 1)
            with engine.Fori(2, B - 2, 2) as i:
                body(i, 0)
                body(i + 1, 1)
            body(B - 2, 0)
            body(B - 1, 1)

        block = ctx.enter_context(nc.Block())

        @block.sync
        def _(sp):
            with nc.allow_non_contiguous_dma(reason="per-channel parameters, a few KB"):
                sp.dma_start(td_sb[:], time_decay.rearrange("(c p) -> p c", p=P)).then_inc(par_in, 16)
                sp.dma_start(tf_sb[:], time_first.rearrange("(c p) -> p c", p=P)).then_inc(par_in, 16)
            sp.dma_start(wg_sb[:], w_gate.rearrange("(c p) e -> p c e", p=P)).then_inc(par_in, 16)
            sp.dma_start(bg_sb[:], b_gate.unsqueeze(0).to_broadcast([P, E])).then_inc(par_in, 16)

            def load_x(b, par):
                for t in range(TT):
                    if not before_start(b, 2):
                        sp.wait_ge(x1_ready, 2 * TT * (b - 2) + TT + t + 1)
                        sp.sem_inc(waited_sp, 1)
                    sp.dma_start(x_sb[:, par, t], x_dram[b, :, t]).then_inc(x_in[par][t], 16)

            def load_v(b, par):
                if not before_start(b, 2):
                    sp.wait_ge(dn_t_ready, CC * (b - 1))
                    sp.sem_inc(waited_sp, 1)
                sp.dma_start(v_sb[:, par], v_dram[b]).then_inc(v_in[par], 16)

            def store_x1(b):
                sp.wait_ge(x1_ready, 2 * TT * (b + 1))
                sp.dma_start(out_dram[b], x1_sb[:]).then_inc(x1_out, 16)

            def store_z(b):
                sp.wait_ge(z_ready, TT * (b + 1))
                sp.dma_start(z_out_dram[b], z_sb[:]).then_inc(z_out, 16)

            def batch(b, par):
                if not is_last(b):
                    load_v(b + 1, 1 - par)
                    load_x(b + 1, 1 - par)
                if not before_start(b, 1):
                    store_x1(b - 1)
                    store_z(b - 1)

            load_x(0, 0)
            load_v(0, 0)
            over_batches(sp, batch)
            store_x1(B - 1)
            store_z(B - 1)
            sp.wait_ge(x1_out, 16 * B)
            sp.wait_ge(z_out, 16 * B)

        @block.gpsimd
        def _(pool):
            nc.gpsimd.memset(ident[:], 0.0).then_inc(ident_zero, 1)
            pool.wait_ge(ident_zero, 1)
            nc.gpsimd.affine_select(out=ident[:], in_=ident[:], compare_op=ALU.not_equal, fill=1.0, base=0,
                                    pattern=[[-1, P]], channel_multiplier=1).then_inc(ident_ready, 1)

            def weigh_values(b, par, t):
                pool.wait_ge(ek_ready, TT * b + t + 1)
                if t == 0:
                    pool.wait_ge(v_in[par], 8 * loads(b, par))
                nc.gpsimd.tensor_tensor(v_sb[:, par, t], ek[:, par, t], v_sb[:, par, t], ALU.mult).then_inc(ekv_ready, 1)

            def quotients(b, pair):
                r = pair % 2
                pool.wait_ge(recip_ready, PAIRS * b + pair + 1)
                nc.gpsimd.tensor_tensor(dn[:, 2 * r:2 * r + 2], dn[:, 2 * r:2 * r + 2],
                                        recip[:, r].unsqueeze(2).to_broadcast([P, 2, 2, T]),
                                        ALU.mult).then_inc(quot_ready, 1)

            def batch(b, par):
                quotients(b, 0)
                quotients(b, 1)
                if not is_last(b):
                    for t in range(TT):
                        weigh_values(b + 1, 1 - par, t)
                quotients(b, 2)
                quotients(b, 3)

            for t in range(TT):
                weigh_values(0, 0, t)
            over_batches(pool, batch)

        @block.scalar
        def _(act):
            nc.scalar.add_instruction(mybir.InstLoadActFuncSet(
                act_func_set_id=EXP_LN_TABLE, name=nc.get_next_instruction_name(),
                engine=mybir.EngineType.Activation))
            act.wait_ge(par_in, 64)
            nc.scalar.activation(decay[:], td_sb[:], ACT.Exp).then_inc(dec_exp, 1)
            act.wait_ge(clipped, 2)
            nc.scalar.activation(scale_a[:], scale_a[:], ACT.Exp, scale=-1.0)
            nc.scalar.activation(scale_b[:], scale_b[:], ACT.Exp)
            act.wait_ge(dec_exp, 1)
            nc.scalar.activation(decay[:], decay[:], ACT.Exp, scale=-1.0).then_inc(params_ready, 1)
            act.wait_ge(eps_set, 1)

            def seed(which, b, order):
                act.wait_ge(mv_ready[which], b + 1)
                nc.scalar.activation(ln_tmp[:, which, 0], mv[:, which, :, 1], ACT.Ln,
                                     bias=eps[:, 0:1]).then_inc(log_done, 1)
                act.wait_ge(log_done, order + 1)
                nc.scalar.activation(ln_tmp[:, which, 1], ln_tmp[:, which, 0], ACT.Exp,
                                     scale=-0.5).then_inc(seed_ready[which], 1)

            def exp_k(b, par, t):
                if t == 0:
                    act.wait_ge(ln_ready[0], b + 1)
                nc.scalar.activation(ek[:, par, t], x_sb[:, par, t], ACT.Exp, bias=shift[:, 0, t:t + 1],
                                     scale=rstd[:, 0, t:t + 1]).then_inc(ek_ready, 1)

            def reciprocal(b, pair):
                r = pair % 2
                act.wait_ge(dn_ready, CC * b + 2 * pair + 2)
                at_least(act, y_ready, PAIRS * b + pair - 1)
                nc.scalar.activation(recip[:, r], dn[:, 2 * r:2 * r + 2, 0], ACT.Ln).then_inc(ln_den, 1)
                act.wait_ge(ln_den, PAIRS * b + pair + 1)
                nc.scalar.activation(recip[:, r], recip[:, r], ACT.Exp, scale=-1.0).then_inc(recip_ready, 1)

            def copy_z_t(b, i):
                t, h = i // 2, i % 2
                act.wait_ge(zt_ready, CC * b + i + 1)
                at_least(act, lg_done, TT * b + t)
                nc.scalar.copy(z_t[:, t % 2, 4 * h:4 * h + 4].rearrange("p c n -> p (c n)"),
                               ps_z[:]).then_inc(zt_copied, 1)

            def scaled_now(b, c):
                act.wait_ge(dn_t_ready, CC * b + c + 1)
                at_least(act, dn_ready, CC * b + c - 3)
                nc.scalar.activation(now[:, c % 4], ps_dn[:, c % 2], ACT.Copy,
                                     scale=scale_b[:, c:c + 1]).then_inc(now_ready, 1)

            def normalise(b, t):
                if t == 0:
                    act.wait_ge(ln_ready[1], b + 1)
                    at_least(act, z_out, 16 * b)
                    at_least(act, zt_ready, CC * b)
                nc.scalar.activation(z_sb[:, t], x1_sb[:, t], ACT.Identity, bias=shift[:, 1, t:t + 1],
                                     scale=rstd[:, 1, t:t + 1]).then_inc(z_ready, 1)

            def batch(b, par):
                has_1, has_2, last = not before_start(b, 1), not before_start(b, 2), is_last(b)

                def copy_z(i):
                    if has_2:
                        copy_z_t(b - 2, i)

                def normalise_tiles(tiles):
                    if has_1:
                        for t in tiles:
                            normalise(b - 1, t)

                def exp_tiles(tiles):
                    if not last:
                        for t in tiles:
                            exp_k(b + 1, 1 - par, t)

                scaled_now(b, 0)
                copy_z(0)
                scaled_now(b, 1)
                copy_z(1)
                scaled_now(b, 2)
                scaled_now(b, 3)
                scaled_now(b, 4)
                reciprocal(b, 0)
                copy_z(2)
                if has_1:
                    seed(1, b - 1, 2 * b)
                copy_z(3)
                reciprocal(b, 1)
                scaled_now(b, 5)
                copy_z(4)
                scaled_now(b, 6)
                copy_z(5)
                if not last:
                    seed(0, b + 1, 2 * b + 1)
                copy_z(6)
                exp_tiles((0, 1))
                copy_z(7)
                normalise_tiles((0,))
                scaled_now(b, 7)
                exp_tiles((2, 3))
                normalise_tiles((1,))
                reciprocal(b, 2)
                normalise_tiles((2, 3))
                reciprocal(b, 3)

            act.wait_ge(params_ready, 1)
            seed(0, 0, 0)
            for t in range(TT):
                exp_k(0, 0, t)
            over_batches(act, batch)
            for i in range(CC):
                copy_z_t(B - 2, i)
                if i == 5:
                    seed(1, B - 1, 2 * B - 1)
            for t in range(TT):
                normalise(B - 1, t)
            for i in range(CC):
                copy_z_t(B - 1, i)

        @block.vector
        def _(dve):
            nc.vector.memset(eps[:], LN_EPS).then_inc(eps_set, 1)
            dve.wait_ge(par_in, 64)
            nc.vector.tensor_scalar(scale_a[:], tf_sb[:], 0.0, None, ALU.max).then_inc(clipped, 1)
            nc.vector.tensor_scalar(scale_b[:], tf_sb[:], 0.0, None, ALU.min).then_inc(clipped, 1)
            BN = 2 * TT
            STEPS = 5

            def stats_of(which, src, t, h):
                return nc.vector.bn_stats(bn[:, which, t, h], src[:, t, h * HALF:(h + 1) * HALF])

            def aggregate(which, b, partial):
                dve.wait_ge(bn_done, partial)
                dve.sem_inc(waited_dve, 1)
                for t in range(TT):
                    last = nc.vector.bn_aggr(mv[:, which, t], bn[:, which, t].rearrange("p h s -> p (h s)"))
                last.then_inc(mv_ready[which], 1)

            def input_stats(b, par):
                for t in range(TT):
                    dve.wait_ge(x_in[par][t], 8 * loads(b, par))
                    for h in range(2):
                        stats_of(0, x_sb[:, par], t, h).then_inc(bn_done, 1)

            def refined(which, b, order):
                tmp = ln_tmp[:, which]
                seed = tmp[:, 1]
                n = STEPS * order
                dve.wait_ge(seed_ready[which], b + 1)
                nc.vector.tensor_tensor(tmp[:, 2], seed, seed, ALU.mult).then_inc(refine, 1)
                nc.vector.tensor_scalar(tmp[:, 3], mv[:, which, :, 1], LN_EPS, None, ALU.add).then_inc(refine, 1)
                dve.wait_ge(refine, n + 2)
                nc.vector.tensor_tensor(tmp[:, 4], tmp[:, 2], tmp[:, 3], ALU.mult).then_inc(refine, 1)
                dve.wait_ge(refine, n + 3)
                nc.vector.tensor_scalar(tmp[:, 5], tmp[:, 4], -0.5, 1.5, ALU.mult, ALU.add).then_inc(refine, 1)
                dve.wait_ge(refine, n + 4)
                nc.vector.tensor_tensor(rstd[:, which], tmp[:, 5], seed, ALU.mult).then_inc(refine, 1)
                dve.wait_ge(refine, n + 5)
                nc.vector.scalar_tensor_tensor(shift[:, which], mv[:, which, :, 0], -1.0, rstd[:, which],
                                               ALU.mult, ALU.mult).then_inc(ln_ready[which], 1)

            def scan(b, c):
                n = CC * b + c
                dve.wait_ge(now_ready, n + 1)
                at_least(dve, dn_ready, n - 1)
                nc.vector.tensor_copy(state[:, c % 2, :, 0:1], ps_dn[:, c % 2, :, 0:1]).then_inc(scan_done, 1)
                for k in range(2):
                    nc.vector.tensor_tensor_scan(
                        state[:, c % 2, k, 1:T + 1], decay[:, c:c + 1].to_broadcast([P, T]), ps_dn[:, c % 2, k],
                        0.0, ALU.mult, ALU.add).then_inc(scan_done, 1)

            def combine(b, c):
                n = CC * b + c
                dve.wait_ge(scan_done, 3 * n + 3)
                if c % 2 == 0:
                    at_least(dve, y_ready, PAIRS * b + c // 2 - 1)
                nc.vector.scalar_tensor_tensor(dn[:, c % 4], state[:, c % 2, :, 0:T], scale_a[:, c:c + 1],
                                               now[:, c % 4], ALU.mult, ALU.add).then_inc(dn_ready, 1)

            def divide(b, pair):
                r = pair % 2
                dve.wait_ge(quot_ready, PAIRS * b + pair + 1)
                nc.vector.scalar_tensor_tensor(neg_y[:, 2 * pair:2 * pair + 2], dn[:, 2 * r:2 * r + 2, 0], -2.0,
                                               dn[:, 2 * r:2 * r + 2, 1], ALU.add, ALU.mult).then_inc(y_ready, 1)

            def residual(b, par, h, t):
                i = TT * h + t
                cols = slice(h * HALF, (h + 1) * HALF)
                if i == 0:
                    at_least(dve, x1_out, 16 * b)
                if h == 0:
                    at_least(dve, z_ready, TT * (b - 1) + t + 1)
                dve.wait_ge(yt_ready, 2 * TT * b + i + 1)
                nc.vector.tensor_tensor(x1_sb[:, t, cols], x_sb[:, par, t, cols], ps_y[:, i % 2],
                                        ALU.subtract).then_inc(x1_ready, 1)

            def output_stats(b, h, t):
                dve.wait_ge(x1_ready, 2 * TT * b + TT * h + t + 1)
                stats_of(1, x1_sb, t, h).then_inc(bn_done, 1)

            def second_half(b, par):
                for t in range(TT):
                    residual(b, par, 1, t)
                    if t:
                        output_stats(b, 1, t - 1)
                output_stats(b, 1, TT - 1)

            def batch(b, par):
                has_1, last = not before_start(b, 1), is_last(b)
                scan(b, 0)
                scan(b, 1)
                combine(b, 0)
                if has_1:
                    divide(b - 1, 3)
                scan(b, 2)
                combine(b, 1)
                if has_1:
                    second_half(b - 1, 1 - par)
                    aggregate(1, b - 1, BN * (2 * b + 1))
                scan(b, 3)
                combine(b, 2)
                scan(b, 4)
                combine(b, 3)
                if has_1:
                    refined(1, b - 1, 2 * b)
                if not last:
                    input_stats(b + 1, 1 - par)
                    aggregate(0, b + 1, BN * (2 * b + 2))
                scan(b, 5)
                if not last:
                    refined(0, b + 1, 2 * b + 1)
                divide(b, 0)
                combine(b, 4)
                scan(b, 6)
                combine(b, 5)
                divide(b, 1)
                scan(b, 7)
                combine(b, 6)
                for t in range(TT):
                    residual(b, par, 0, t)
                    if t == 1:
                        combine(b, 7)
                    if t > 1:
                        output_stats(b, 0, t - 2)
                output_stats(b, 0, TT - 2)
                output_stats(b, 0, TT - 1)
                divide(b, 2)

            input_stats(0, 0)
            aggregate(0, 0, BN)
            refined(0, 0, 0)
            dve.wait_ge(params_ready, 1)
            over_batches(dve, batch)
            divide(B - 1, 3)
            second_half(B - 1, 1)
            aggregate(1, B - 1, BN * 2 * B)
            refined(1, B - 1, 2 * B - 1)
            dve.wait_ge(lg_done, TT * B + 1)
            nc.vector.tensor_tensor(logits[:], ps_lg[:, 0:TT * B * E].rearrange("p (n e) -> p e n", e=E),
                                    bg_sb[:].unsqueeze(2).to_broadcast([P, E, TT * B]), ALU.add).then_inc(logits_out, 1)
            dve.wait_ge(logits_out, 1)

        @block.tensor
        def _(pe):
            pe.wait_ge(ident_ready, 1)
            pe.wait_ge(par_in, 64)
            pe.sem_inc(lg_done, 1)

            def transpose_z(b, i):
                t, h = i // 2, i % 2
                pe.wait_ge(z_ready, TT * b + t + 1)
                at_least(pe, zt_copied, CC * b + i)
                for c in range(4):
                    last = nc.tensor.transpose(ps_z[:, c * P:(c + 1) * P],
                                               z_sb[:, t, (4 * h + c) * P:(4 * h + c + 1) * P], ident[:])
                last.then_inc(zt_ready, 1)

            def route(b, t):
                pe.wait_ge(zt_copied, CC * b + 2 * t + 2)
                col = E * (TT * b + t)
                for c in range(CC):
                    last = nc.tensor.matmul(ps_lg[:, bass.ds(col, E)], z_t[:, t % 2, c], wg_sb[:, c],
                                            start=(c == 0), stop=(c == CC - 1))
                last.then_inc(lg_done, 1)

            def transpose_chunk(b, par, c):
                at_least(pe, scan_done, 3 * (CC * b + c - 1))
                at_least(pe, now_ready, CC * b + c - 1)
                for k, src in enumerate((ek, v_sb)):
                    for t in range(TT):
                        last = nc.tensor.transpose(ps_dn[:, c % 2, k, t * P:(t + 1) * P],
                                                   src[:, par, t, c * P:(c + 1) * P], ident[:])
                last.then_inc(dn_t_ready, 1)

            def transpose_y(b, h):
                pe.wait_ge(y_ready, PAIRS * b + PAIRS // 2 * (h + 1))
                for t in range(TT):
                    i = TT * h + t
                    at_least(pe, x1_ready, 2 * TT * b + i - 1)
                    for c in range(4):
                        last = nc.tensor.transpose(ps_y[:, i % 2, c * P:(c + 1) * P],
                                                   neg_y[:, 4 * h + c, t * P:(t + 1) * P], ident[:])
                    last.then_inc(yt_ready, 1)

            def batch(b, par):
                has_1, has_2 = not before_start(b, 1), not before_start(b, 2)
                pe.wait_ge(ekv_ready, TT * (b + 1))
                for c in range(CC):
                    transpose_chunk(b, par, c)
                    if has_1 and c == 3:
                        transpose_y(b - 1, 1)
                    if has_2:
                        if c == 6:
                            route(b - 2, 1)
                        for i in ((0,), (1,), (), (), (2, 3), (4,), (5, 6, 7), ())[c]:
                            transpose_z(b - 2, i)
                            if i in (2, 6):
                                route(b - 2, i // 2 - 1)
                        if c == CC - 1:
                            route(b - 2, TT - 1)
                transpose_y(b, 0)

            over_batches(pe, batch)
            for b in (B - 2, B - 1):
                for i in range(CC):
                    transpose_z(b, i)
                    if i in (2, 4, 6):
                        route(b, i // 2 - 1)
                    if b == B - 2 and i == 4:
                        transpose_y(B - 1, 1)
                route(b, TT - 1)


def feed_forward(nc, w1, w2, z_dram, out_rows, logits, ident):
    E, D, H = w1.shape
    N = z_dram.shape[0]
    NT = N // P
    CAP = N // E
    ST = CAP // P
    KD = D // P
    HALF = 512
    DH = D // HALF
    BLOCKS = 2
    GROUPS = H // (P * BLOCKS)
    NB = GROUPS * BLOCKS
    TILES = ST * DH
    DIGIT = 4
    ROUNDS = 15
    LIMBS = 5

    w1_v = w1.rearrange("e (k p) (g n) -> e g p k n", p=P, n=P * BLOCKS)
    w2_v = w2.rearrange("e (g b p) n -> e g p b n", p=P, b=BLOCKS)

    with ExitStack() as ctx:
        def sb(name, shape, dt=F32, stack=ctx):
            return stack.enter_context(nc.sbuf_tensor(name, shape, dt))

        def ps(name, shape, dt=F32):
            return ctx.enter_context(nc.psum_tensor(name, shape, dt))

        def sem(name):
            return ctx.enter_context(nc.semaphore(name))

        x_hi = sb("x_hi", [P, KD, CAP], F32R)
        x_lo = sb("x_lo", [P, KD, CAP], F32R)
        h_hi = sb("h_hi", [P, 2, BLOCKS, CAP], F32R)
        h_lo = sb("h_lo", [P, 2, BLOCKS, CAP], F32R)
        h_sb = sb("h_sb", [P, CAP])
        w1_hi = sb("w1_hi", [P, 2, KD, P], F32R)
        w1_lo = sb("w1_lo", [P, 2, KD, P], F32R)
        w2_hi = sb("w2_hi", [P, 2, BLOCKS, D], F32R)
        w2_lo = sb("w2_lo", [P, 2, BLOCKS, D], F32R)
        w1_raw = sb("w1_raw", [P, KD, P * BLOCKS])
        w2_raw = sb("w2_raw", [P, BLOCKS, D])
        x_raw = sb("x_raw", [P, 2, D])
        index = sb("index", [P, E, ST], U32)
        weight_now = sb("weight_now", [P, ST])
        weight = sb("weight", [P, E, ST])

        scratch = ExitStack()
        token_hot = sb("token_hot", [P, 2, NT, P], BF16, scratch)
        slot_hot = sb("slot_hot", [P, NT, ST], BF16, scratch)
        payload = sb("payload", [P, NT, LIMBS, ST], BF16, scratch)
        over = sb("over", [P, E, DIGIT, NT], F32, scratch)
        score = sb("score", [P, E, NT], F32, scratch)
        expd = sb("expd", [P, E, NT], F32, scratch)
        wins = sb("wins", [P, E, NT], F32, scratch)
        beats = sb("beats", [P, 3, 3, NT], F32, scratch)
        t0 = sb("t0", [P, E, NT], F32, scratch)
        t1 = sb("t1", [P, E, NT], F32, scratch)
        t2 = sb("t2", [P, E, NT], F32, scratch)
        t3 = sb("t3", [P, E, NT], F32, scratch)
        best = sb("best", [P, NT], F32, scratch)
        total = sb("total", [P, NT], F32, scratch)
        cand = sb("cand", [P, E, DIGIT], U32, scratch)
        kept = sb("kept", [P, E, DIGIT], F32, scratch)
        digits = sb("digits", [P, DIGIT], U32, scratch)
        cut = sb("cut", [P, E], U32, scratch)
        counts = sb("counts", [P, E, DIGIT], BF16, scratch)
        masks = sb("masks", [P, 2, E, NT], BF16, scratch)
        slot_u = sb("slot_u", [P, 2, E, NT], U32, scratch)
        slot_f = sb("slot_f", [P, 2, E, NT], F32, scratch)
        limbs = sb("limbs", [P, 3, E, NT], BF16, scratch)
        iota_u = sb("iota_u", [P, P], U32, scratch)
        iota_f = sb("iota_f", [P, P], F32, scratch)
        part_u = sb("part_u", [P, 1], U32, scratch)
        ones = sb("ones", [P, P], BF16, scratch)
        before = sb("before", [P, P], BF16, scratch)
        picked = sb("picked", [P, LIMBS, ST], F32, scratch)
        tok_f = sb("tok_f", [P, 2, ST], F32, scratch)
        need = sb("need", [P, E], F32, scratch)
        scratch.close()
        acc = sb("acc", [P, ST, D])

        ps_h = ps("ps_h", [P, 2, CAP])
        ps_y = ps("ps_y2", [P, 2, HALF])
        ps_x = ps("ps_x", [P, 2, HALF])

        w1_in, w2_in = sem("w1_in"), sem("w2_in")
        w1_hi_done, w1_lo_done = sem("w1_hi_done"), sem("w1_lo_done")
        w2_hi_done, w2_lo_done = sem("w2_hi_done"), sem("w2_lo_done")
        step = sem("step")
        const_done = sem("const_done")
        expd_ready = sem("expd_ready")
        exp_in = sem("exp_in")
        counted = sem("counted")
        counts_ready = sem("counts_ready")
        masks_ready = sem("masks_ready")
        prefix_ready = sem("prefix_ready")
        hot_ready = sem("hot_ready")
        slots_ready = sem("slots_ready")
        index_ready = sem("index_ready")
        first_in = [sem(f"first_in{s}") for s in range(ST)]
        x_raw_in = [sem("x_raw_in0"), sem("x_raw_in1")]
        x_t_ready = sem("x_t_ready")
        x_hi_done = sem("x_hi_done")
        x_lo_done = sem("x_lo_done")
        h_mm_done = sem("h_mm_done")
        gelu_done = sem("gelu_done")
        h_hi_done, h_lo_done = sem("h_hi_done"), sem("h_lo_done")
        y_mm_done = sem("y_mm_done")
        y_added = sem("y_added")
        weight_set = sem("weight_set")
        scattered = sem("scattered")
        acc_free = sem("acc_free")

        def over_groups(engine, body):
            body(0, 0)
            body(1, 1)
            with engine.Fori(2, GROUPS - 2, 2) as i:
                body(i, 0)
                body(i + 1, 1)
            body(GROUPS - 2, 0)
            body(GROUPS - 1, 1)

        def first_rows(s):
            assert CAP == D and ST == 4 * BLOCKS
            part = (h_hi, h_lo)[s // 4]
            return part[:, s // 2 % 2, s % 2].bitcast(F32)

        def hot_operands(e):
            return (iota_f[:].unsqueeze(1).to_broadcast([P, NT, P]),
                    slot_f[:, 0, e].unsqueeze(2).to_broadcast([P, NT, P]))

        block = ctx.enter_context(nc.Block())

        @block.sync
        def _(sp):
            def load(e, g):
                done = NB * e + BLOCKS * g
                at_least(sp, w1_hi_done, done)
                at_least(sp, w1_lo_done, done)
                sp.dma_start(w1_raw[:], w1_v[e, g]).then_inc(w1_in, 16)
                at_least(sp, w2_hi_done, done)
                at_least(sp, w2_lo_done, done)
                sp.dma_start(w2_raw[:], w2_v[e, g]).then_inc(w2_in, 16)

            load(0, 0)
            with sp.Fori(1, GROUPS) as g:
                load(0, g)
            with sp.Fori(1, E) as e:
                with sp.Fori(0, GROUPS) as g:
                    load(e, g)

        @block.gpsimd
        def _(pool):
            nc.gpsimd.iota(iota_u[:], [[1, P]], base=0, channel_multiplier=0).then_inc(const_done, 1)
            nc.gpsimd.iota(part_u[:], [[1, 1]], base=0, channel_multiplier=1).then_inc(const_done, 1)
            nc.gpsimd.iota(digits[:], [[1, DIGIT]], base=0, channel_multiplier=0).then_inc(const_done, 1)
            nc.gpsimd.memset(ones[:], 1.0).then_inc(const_done, 1)
            pool.wait_ge(const_done, 4)
            nc.gpsimd.affine_select(out=before[:], in_=ones[:], compare_op=ALU.is_gt, fill=0.0, base=0,
                                    pattern=[[1, P]], channel_multiplier=-1).then_inc(const_done, 1)

            def gather(e, s):
                n = ST * e + s
                at_least(pool, x_t_ready, 2 * (n - 1))
                nc.gpsimd.indirect_dma_start(
                    x_raw[:, s % 2], None, z_dram,
                    bass.IndirectOffsetOnAxis(ap=index[:, e, s:s + 1], axis=0)).then_inc(x_raw_in[s % 2], 16)

            def scatter(e, s):
                pool.wait_ge(y_added, 2 + TILES * (GROUPS * e + GROUPS - 1) + DH * (s + 1))
                nc.gpsimd.indirect_dma_start(
                    out_rows, bass.IndirectOffsetOnAxis(ap=index[:, e, s:s + 1], axis=0),
                    acc[:, s], None, compute_op=ALU.add).then_inc(scattered, 16)

            pool.wait_ge(index_ready, 1)
            for s in range(ST):
                nc.gpsimd.indirect_dma_start(
                    first_rows(s), None, z_dram,
                    bass.IndirectOffsetOnAxis(ap=index[:, 0, s:s + 1], axis=0)).then_inc(first_in[s], 16)
            pool.wait_ge(index_ready, E)
            for e in range(E):
                at_least(pool, scattered, 16 * ST * e)
                pool.sem_inc(acc_free, 1)
                if e + 1 < E:
                    gather(e + 1, 0)
                    gather(e + 1, 1)
                for s in range(ST):
                    if e + 1 < E and s + 2 < ST:
                        gather(e + 1, s + 2)
                    scatter(e, s)
            pool.wait_ge(scattered, 16 * ST * E)

        @block.scalar
        def _(act):
            def split_w1(n, b, first=False):
                act.wait_ge(w1_in, 8 * (n - b) + 16)
                at_least(act, h_mm_done, n)
                nc.scalar.copy(w1_hi[:, b], w1_raw[:, :, b * P:(b + 1) * P]).then_inc(w1_hi_done, 1)

            def split_w2(n, b, par):
                act.wait_ge(w2_in, 8 * (n - b) + 16)
                nc.scalar.copy(w2_hi[:, par, b], w2_raw[:, b]).then_inc(w2_hi_done, 1)

            def split_x(e, s):
                for h in range(2):
                    act.wait_ge(x_t_ready, 2 * ST * e + 2 * s + h + 1)
                    nc.scalar.copy(x_hi[:, 4 * h:4 * h + 4, s * P:(s + 1) * P],
                                   ps_x[:, h].rearrange("p (k n) -> p k n", n=P)).then_inc(x_hi_done, 1)

            def expert(e):
                last_expert = isinstance(e, int) and e == E - 1

                def group(g, par):
                    for b in range(BLOCKS):
                        n = NB * e + BLOCKS * g + b
                        if not (last_expert and isinstance(g, int) and g == GROUPS - 1 and b == BLOCKS - 1):
                            split_w1(n + 1, 1 - b)
                        act.wait_ge(h_mm_done, n + 2)
                        act.wait_ge(h_lo_done, n + 1)
                        nc.scalar.activation(h_sb[:], ps_h[:, b], ACT.Gelu).then_inc(gelu_done, 1)
                        split_w2(n, b, par)
                        act.wait_ge(gelu_done, n + 1)
                        nc.scalar.copy(h_hi[:, par, b], h_sb[:]).then_inc(h_hi_done, 1)

                over_groups(act, group)

            act.wait_ge(exp_in, 1)
            nc.scalar.activation(expd[:], t0[:], ACT.Exp).then_inc(expd_ready, 1)
            split_w1(0, 0)
            for s in range(ST):
                split_x(0, s)
            with act.Fori(0, E - 1) as e:
                expert(e)
                for s in range(ST):
                    split_x(e + 1, s)
            expert(E - 1)

        @block.vector
        def _(dve):
            made = [0]

            def then(instruction):
                made[0] += 1
                instruction.then_inc(step, 1)
                dve.wait_ge(step, made[0])

            def tt(o, a, b, op):
                return nc.vector.tensor_tensor(o, a, b, op)

            dve.wait_ge(const_done, 5)
            for e in range(E - 1):
                last = tt(beats[:, e, e:], logits[:, e:e + 1].to_broadcast([P, E - 1 - e, NT]), logits[:, e + 1:],
                          ALU.is_ge)
            then(last)
            then(tt(t1[:, 0:2], logits[:, 0:2], logits[:, 2:4], ALU.max))
            then(tt(best[:], t1[:, 0], t1[:, 1], ALU.max))
            then(tt(t0[:], logits[:], best[:].unsqueeze(1).to_broadcast([P, E, NT]), ALU.subtract))
            nc.vector.engine_nop().then_inc(exp_in, 1)
            g = lambda e, f: beats[:, e, f - 1]
            then(tt(t1[:, 0], g(0, 1), g(0, 2), ALU.add))
            then(tt(wins[:, 0], t1[:, 0], g(0, 3), ALU.add))
            then(tt(t1[:, 1], g(1, 2), g(1, 3), ALU.add))
            then(tt(t2[:, 1], t1[:, 1], g(0, 1), ALU.subtract))
            then(nc.vector.tensor_scalar(wins[:, 1], t2[:, 1], 1.0, None, ALU.add))
            then(tt(t1[:, 2], g(2, 3), g(0, 2), ALU.subtract))
            then(tt(t2[:, 2], t1[:, 2], g(1, 2), ALU.subtract))
            then(nc.vector.tensor_scalar(wins[:, 2], t2[:, 2], 2.0, None, ALU.add))
            then(tt(t1[:, 3], g(0, 3), g(1, 3), ALU.add))
            then(tt(t2[:, 3], t1[:, 3], g(2, 3), ALU.add))
            then(nc.vector.tensor_scalar(wins[:, 3], t2[:, 3], -1.0, 3.0, ALU.mult, ALU.add))
            dve.wait_ge(expd_ready, 1)
            then(nc.vector.scalar_tensor_tensor(t1[:], wins[:], float(E - TOPK), expd[:], ALU.is_ge, ALU.mult))
            then(tt(t2[:, 0:2], t1[:, 0:2], t1[:, 2:4], ALU.add))
            then(tt(total[:], t2[:, 0], t2[:, 1], ALU.add))
            then(nc.vector.reciprocal(best[:], total[:]))
            then(tt(score[:], t1[:], best[:].unsqueeze(1).to_broadcast([P, E, NT]), ALU.mult))
            then(nc.vector.memset(cut[:], 0))
            then(nc.vector.tensor_scalar(digits[:], digits[:], 2 * (ROUNDS - 1), None, ALU.logical_shift_left))
            SEARCH = 5
            base = made[0]
            cut_f, cand_f = cut[:].bitcast(F32), cand[:].bitcast(F32)
            with dve.Fori(0, ROUNDS) as i:
                done = base + SEARCH * i
                dve.wait_ge(step, done)
                tt(cand[:], cut[:].unsqueeze(2).to_broadcast([P, E, DIGIT]),
                   digits[:].unsqueeze(1).to_broadcast([P, E, DIGIT]), ALU.bitwise_or).then_inc(step, 1)
                dve.wait_ge(step, done + 1)
                tt(over[:], score[:].unsqueeze(2).to_broadcast([P, E, DIGIT, NT]),
                   cand_f.unsqueeze(3).to_broadcast([P, E, DIGIT, NT]), ALU.is_ge).then_inc(step, 1)
                dve.wait_ge(step, done + 2)
                with nc.allow_low_precision(reason="counts up to 32 are exact in bfloat16"):
                    nc.vector.tensor_reduce(counts[:], over[:], AX_X, ALU.add).then_inc(counts_ready, 1)
                nc.vector.tensor_scalar(digits[:], digits[:], 2, None, ALU.logical_shift_right).then_inc(step, 1)
                dve.wait_ge(step, done + 3)
                dve.wait_ge(counted, i + 1)
                nc.vector.scalar_tensor_tensor(
                    kept[:].rearrange("p e d -> p (e d)"), ps_x[:, 0, 0:E * DIGIT], float(CAP) - 0.5,
                    cand_f.rearrange("p e d -> p (e d)"), ALU.is_ge, ALU.mult).then_inc(step, 1)
                dve.wait_ge(step, done + 4)
                nc.vector.tensor_reduce(cut_f, kept[:], AX_X, ALU.max).then_inc(step, 1)
            made[0] = base + SEARCH * ROUNDS
            dve.wait_ge(step, made[0])
            cut_b = cut_f.unsqueeze(2).to_broadcast([P, E, NT])
            tt(masks[:, 0], score[:], cut_b, ALU.is_gt)
            then(tt(masks[:, 1], score[:], cut_b, ALU.is_equal))
            nc.vector.engine_nop().then_inc(masks_ready, 1)

            EN = E * NT
            dve.wait_ge(prefix_ready, 1)
            within = ps_h[:, 0, 0:2 * EN].rearrange("p (m e n) -> p m e n", m=2, e=E)
            totals = ps_h[:, 1, 0:2 * EN].rearrange("p (m e n) -> p m e n", m=2, e=E)
            for m, t in ((0, t0), (1, t1)):
                for e in range(E):
                    last = nc.vector.tensor_tensor_scan(t[:, e], ones[:, 0:1].to_broadcast([P, NT]),
                                                        totals[:, m, e], 0.0, ALU.mult, ALU.add)
            then(last)
            then(nc.vector.tensor_scalar(need[:], t0[:, :, NT - 1], -1.0, float(CAP), ALU.mult, ALU.add))
            then(tt(t2[:], t0[:], totals[:, 0], ALU.subtract))
            then(tt(t3[:], t2[:], within[:, 0], ALU.add))
            then(tt(t2[:], t1[:], totals[:, 1], ALU.subtract))
            then(tt(t0[:], t2[:], within[:, 1], ALU.add))
            need_b = need[:].unsqueeze(2).to_broadcast([P, E, NT])
            then(tt(t1[:], t0[:], need_b, ALU.is_lt))
            then(tt(t2[:], t1[:], masks[:, 1], ALU.mult))
            then(tt(wins[:], t2[:], masks[:, 0], ALU.add))
            then(tt(t1[:], t0[:], need_b, ALU.min))
            then(tt(t2[:], t3[:], t1[:], ALU.add))
            then(nc.vector.tensor_scalar(t1[:], wins[:], float(-N), float(N), ALU.mult, ALU.add))
            then(tt(slot_u[:, 0], t2[:], t1[:], ALU.add))
            then(nc.vector.tensor_scalar(slot_u[:, 1], slot_u[:, 0], P.bit_length() - 1, None,
                                         ALU.logical_shift_right))
            then(nc.vector.tensor_scalar(slot_u[:, 0], slot_u[:, 0], P - 1, None, ALU.bitwise_and))
            nc.vector.tensor_copy(slot_f[:], slot_u[:])
            nc.vector.tensor_copy(iota_f[:], iota_u[:])
            then(nc.vector.tensor_copy(limbs[:, 0], score[:]))
            then(tt(t1[:], score[:], limbs[:, 0], ALU.subtract))
            then(nc.vector.tensor_copy(limbs[:, 1], t1[:]))
            then(tt(t2[:], t1[:], limbs[:, 1], ALU.subtract))
            then(nc.vector.tensor_copy(limbs[:, 2], t2[:]))

            def one_hot(e):
                at_least(dve, slots_ready, e - 1)
                then(tt(token_hot[:, e % 2], *hot_operands(e), ALU.is_equal))

            def payloads(e):
                at_least(dve, slots_ready, e)
                then(tt(slot_hot[:], iota_f[:, 0:ST].unsqueeze(1).to_broadcast([P, NT, ST]),
                        slot_f[:, 1, e].unsqueeze(2).to_broadcast([P, NT, ST]), ALU.is_equal))
                tt(payload[:, :, 0], slot_hot[:], iota_f[:, 0:NT].unsqueeze(2).to_broadcast([P, NT, ST]), ALU.mult)
                tt(payload[:, :, 1], slot_hot[:], part_u[:].unsqueeze(2).to_broadcast([P, NT, ST]), ALU.mult)
                for k in range(3):
                    last = tt(payload[:, :, 2 + k], slot_hot[:],
                              limbs[:, k, e].unsqueeze(2).to_broadcast([P, NT, ST]), ALU.mult)
                last.then_inc(hot_ready, 1)

            def read_lists(e):
                dve.wait_ge(slots_ready, e + 1)
                then(nc.vector.tensor_copy(picked[:].rearrange("p l s -> p (l s)"), ps_y[:, e % 2, 0:LIMBS * ST]))
                nc.vector.tensor_scalar(tok_f[:, 0], picked[:, 0], float(P), None, ALU.mult)
                then(tt(tok_f[:, 1], picked[:, 2], picked[:, 3], ALU.add))
                then(tt(index[:, e], tok_f[:, 0], picked[:, 1], ALU.add))
                nc.vector.engine_nop().then_inc(index_ready, 1)
                then(tt(weight[:, e], tok_f[:, 1], picked[:, 4], ALU.add))

            def split_w1(n, b):
                dve.wait_ge(w1_hi_done, n + 1)
                tt(w1_lo[:, b], w1_raw[:, :, b * P:(b + 1) * P], w1_hi[:, b].bitcast(F32),
                   ALU.subtract).then_inc(w1_lo_done, 1)

            def split_w2(n, b, par, half):
                cols = slice(half * HALF, (half + 1) * HALF)
                if half == 0:
                    dve.wait_ge(w2_hi_done, n + 1)
                low = tt(w2_lo[:, par, b, cols], w2_raw[:, b, cols], w2_hi[:, par, b, cols].bitcast(F32), ALU.subtract)
                if half == 1:
                    low.then_inc(w2_lo_done, 1)

            def split_h(n, b, par, half):
                cols = slice(half * HALF, (half + 1) * HALF)
                if half == 0:
                    dve.wait_ge(h_hi_done, n + 1)
                low = tt(h_lo[:, par, b, cols], h_sb[:, cols], h_hi[:, par, b, cols].bitcast(F32), ALU.subtract)
                if half == 1:
                    low.then_inc(h_lo_done, 1)

            def split_x(e, s):
                for h in range(2):
                    dve.wait_ge(x_hi_done, 2 * ST * e + 2 * s + h + 1)
                    cols = slice(s * P, (s + 1) * P)
                    tt(x_lo[:, 4 * h:4 * h + 4, cols], ps_x[:, h].rearrange("p (k n) -> p k n", n=P),
                       x_hi[:, 4 * h:4 * h + 4, cols].bitcast(F32), ALU.subtract).then_inc(x_lo_done, 1)

            def add_y(e, g, tile):
                s, dh = tile // DH, tile % DH
                a = acc[:, s, dh * HALF:(dh + 1) * HALF]
                if isinstance(g, int) and g == 0:
                    if tile == 0:
                        dve.wait_ge(acc_free, e + 1)
                    dve.wait_ge(y_mm_done, TILES * (GROUPS * e + g) + tile + 1)
                    nc.vector.tensor_scalar(a, ps_y[:, tile % 2], weight_now[:, s:s + 1], None,
                                            ALU.mult).then_inc(y_added, 1)
                    return
                dve.wait_ge(y_mm_done, TILES * (GROUPS * e + g) + tile + 1)
                nc.vector.scalar_tensor_tensor(a, ps_y[:, tile % 2], weight_now[:, s:s + 1], a, ALU.mult,
                                               ALU.add).then_inc(y_added, 1)

            def expert(e):
                last_expert = isinstance(e, int) and e == E - 1

                def group(g, par):
                    first = isinstance(g, int) and g == 0
                    for b in range(BLOCKS):
                        n = NB * e + BLOCKS * g + b
                        if not (last_expert and isinstance(g, int) and g == GROUPS - 1 and b == BLOCKS - 1):
                            split_w1(n + 1, 1 - b)
                        tiles = [] if first else list(range(b * TILES // 2, (b + 1) * TILES // 2))
                        splits = [(split_h, 0), (split_h, 1), (split_w2, 0), (split_w2, 1)]
                        for at, tile in enumerate(tiles):
                            add_y(e, g - 1, tile)
                            if 1 <= at <= len(splits):
                                split, half = splits[at - 1]
                                split(n, b, par, half)
                        if not tiles:
                            for split, half in splits:
                                split(n, b, par, half)

                over_groups(dve, group)

            dve.sem_inc(h_lo_done, 1)
            one_hot(0)
            payloads(0)
            read_lists(0)
            one_hot(1)
            split_x(0, 0)
            payloads(1)
            split_x(0, 1)
            read_lists(1)
            one_hot(2)
            split_x(0, 2)
            split_x(0, 3)
            payloads(2)
            split_x(0, 4)
            read_lists(2)
            split_x(0, 5)
            one_hot(3)
            split_x(0, 6)
            payloads(3)
            split_x(0, 7)
            split_w1(0, 0)
            read_lists(3)
            dve.sem_inc(y_added, 2)

            def take_weights(e):
                dve.wait_ge(y_added, 2 + TILES * GROUPS * e)
                nc.vector.tensor_copy(weight_now[:], weight[:, e]).then_inc(weight_set, 1)
                dve.wait_ge(weight_set, e + 1)

            with dve.Fori(0, E - 1) as e:
                take_weights(e)
                expert(e)
                for s in range(ST):
                    split_x(e + 1, s)
                    for dh in range(DH):
                        add_y(e, GROUPS - 1, DH * s + dh)
            take_weights(E - 1)
            expert(E - 1)
            for tile in range(TILES):
                add_y(E - 1, GROUPS - 1, tile)

        @block.tensor
        def _(pe):
            pe.wait_ge(const_done, 5)
            with pe.Fori(0, ROUNDS) as i:
                pe.wait_ge(counts_ready, i + 1)
                nc.tensor.matmul(ps_x[:, 0, 0:E * DIGIT], ones[:], counts[:].rearrange("p e d -> p (e d)"),
                                 start=True, stop=True).then_inc(counted, 1)
            pe.wait_ge(masks_ready, 1)
            flat = masks[:].rearrange("p m e n -> p (m e n)")
            nc.tensor.matmul(ps_h[:, 0, 0:2 * E * NT], before[:], flat, start=True, stop=True)
            nc.tensor.matmul(ps_h[:, 1, 0:2 * E * NT], ones[:], flat, start=True, stop=True).then_inc(prefix_ready, 1)

            def lists(e):
                pe.wait_ge(hot_ready, e + 1)
                at_least(pe, index_ready, e - 1)
                for j in range(NT):
                    last = nc.tensor.matmul(ps_y[:, e % 2, 0:LIMBS * ST], token_hot[:, e % 2, j],
                                            payload[:, j].rearrange("p l s -> p (l s)"),
                                            start=(j == 0), stop=(j == NT - 1))
                last.then_inc(slots_ready, 1)

            def transpose_x(e, s):
                first = isinstance(e, int)
                rows = first_rows(s) if first else x_raw[:, s % 2]
                if first:
                    pe.wait_ge(first_in[s], 16)
                else:
                    pe.wait_ge(x_raw_in[s % 2], 16 * (ST // 2) * (e - 1) + 16 * (s // 2 + 1))
                for h in range(2):
                    at_least(pe, x_lo_done, 2 * ST * e + 2 * s + h - 1)
                    for k in range(4):
                        last = nc.tensor.transpose(ps_x[:, h, k * P:(k + 1) * P],
                                                   rows[:, (4 * h + k) * P:(4 * h + k + 1) * P], ident[:])
                    last.then_inc(x_t_ready, 1)

            def product(out, hi_lo_l, hi_lo_r, k, count, first, stop):
                (lh, ll), (rh, rl) = hi_lo_l, hi_lo_r
                nc.tensor.matmul(out, lh, rh, start=first, stop=False)
                nc.tensor.matmul(out, lh, rl, start=False, stop=False)
                return nc.tensor.matmul(out, ll, rh, start=False, stop=stop)

            def hidden(e, g, b):
                n = NB * e + BLOCKS * g + b
                pe.wait_ge(w1_hi_done, n + 1)
                pe.wait_ge(w1_lo_done, n + 1)
                for half in range(2):
                    cols = slice(half * HALF, (half + 1) * HALF)
                    for k in range(KD):
                        last = product(ps_h[:, b, cols], (w1_hi[:, b, k], w1_lo[:, b, k]),
                                       (x_hi[:, k, cols], x_lo[:, k, cols]), k, KD, k == 0, k == KD - 1)
                last.then_inc(h_mm_done, 1)

            def outputs(e, g, par, tile):
                n = GROUPS * e + g
                s, dh = tile // DH, tile % DH
                if tile == 0:
                    for done in (h_hi_done, w2_hi_done, w2_lo_done):
                        pe.wait_ge(done, BLOCKS * (n + 1))
                    pe.wait_ge(h_lo_done, BLOCKS * (n + 1) + 1)
                pe.wait_ge(y_added, TILES * n + tile + 1)
                rows, cols = slice(s * P, (s + 1) * P), slice(dh * HALF, (dh + 1) * HALF)
                for b in range(BLOCKS):
                    last = product(ps_y[:, tile % 2], (h_hi[:, par, b, rows], h_lo[:, par, b, rows]),
                                   (w2_hi[:, par, b, cols], w2_lo[:, par, b, cols]), b, BLOCKS, b == 0,
                                   b == BLOCKS - 1)
                last.then_inc(y_mm_done, 1)

            def expert(e):
                pe.wait_ge(x_lo_done, 2 * ST * (e + 1))

                def group(g, par):
                    for b in range(BLOCKS):
                        hidden(e, g, b)
                        if not (isinstance(g, int) and g == 0):
                            for tile in range(b * TILES // 2, (b + 1) * TILES // 2):
                                outputs(e, g - 1, 1 - par, tile)

                over_groups(pe, group)

            pe.sem_inc(h_mm_done, 1)
            lists(0)
            for s in range(ST):
                transpose_x(0, s)
                if s in (1, 4, 7):
                    lists((s + 2) // 3)
            with pe.Fori(0, E - 1) as e:
                expert(e)
                for s in range(ST):
                    transpose_x(e + 1, s)
                    for dh in range(DH):
                        outputs(e, GROUPS - 1, (GROUPS - 1) % 2, DH * s + dh)
            expert(E - 1)
            for tile in range(TILES):
                outputs(E - 1, GROUPS - 1, (GROUPS - 1) % 2, tile)


def build(nc, x, ctx_2048, L0_xattn_time_decay, L0_xattn_time_first, L0_ffn_Wg, L0_ffn_bg, L0_ffn_W1, L0_ffn_W2, out):
    B, T, C = x.shape
    E = L0_ffn_Wg.shape[1]
    z_dram = nc.dram_tensor("z_rows", (B * T, C), F32, kind="Internal").ap()
    with nc.sbuf_tensor("logits", [P, E, B * T // P], F32) as logits, nc.sbuf_tensor("ident", [P, P], F32) as ident:
        token_mixing(nc, x, ctx_2048, L0_xattn_time_decay, L0_xattn_time_first, L0_ffn_Wg, L0_ffn_bg, out, z_dram,
                     logits, ident)
        feed_forward(nc, L0_ffn_W1, L0_ffn_W2, z_dram, out.rearrange("b t c -> (b t) c"), logits, ident)


_INS = ['x', 'ctx_2048', 'L0_xattn_time_decay', 'L0_xattn_time_first', 'L0_ffn_Wg', 'L0_ffn_bg', 'L0_ffn_W1',
        'L0_ffn_W2']


def kernel(**inputs):
    import numpy as _np
    import concourse.bacc as _bacc
    from concourse import mybir as _mybir
    from concourse.bass_utils import run_bass_kernel_spmd as _run

    nc = _bacc.Bacc("TRN2", target_bir_lowering=False, num_devices=1)
    arrays, args = {}, []
    for name in _INS:
        a = _np.ascontiguousarray(inputs[name])
        arrays[f"in_{name}_dram"] = a
        args.append(nc.dram_tensor(f"in_{name}_dram", a.shape, _mybir.dt.from_np(a.dtype), kind="ExternalInput").ap())
    out = nc.dram_tensor("out_0_dram", inputs["x"].shape, _mybir.dt.float32, kind="ExternalOutput").ap()
    build(nc, *args, out)
    r = _run(nc, [arrays], core_ids=[0])
    return r.results[0]["out_0_dram"]
```

```python
from contextlib import ExitStack

import concourse.bass as bass
from concourse import mybir

P = 128
F32 = mybir.dt.float32
F32R = mybir.dt.float32r
BF16 = mybir.dt.bfloat16
U32 = mybir.dt.uint32
ALU = mybir.AluOpType
ACT = mybir.ActivationFunctionType
AX_X = mybir.AxisListType.X

LN_EPS = 1e-5
EXP_LN_TABLE = 6
TOPK = 2


def at_least(engine, semaphore, value):
    if isinstance(value, int) and value <= 0:
        return
    engine.wait_ge(semaphore, value)


def token_mixing(nc, x, v, time_decay, time_first, w_gate, b_gate, out, z_dram, logits, ident):
    B, T, C = x.shape
    TT = T // P
    CC = C // P
    E = w_gate.shape[1]
    HALF = 512
    PAIRS = CC // 2

    x_dram = x.rearrange("b (t p) c -> b p t c", p=P)
    v_dram = v.rearrange("b (t p) c -> b p t c", p=P)
    out_dram = out.rearrange("b (t p) c -> b p t c", p=P)
    z_out_dram = z_dram.rearrange("(b t p) c -> b p t c", p=P, t=TT)

    with ExitStack() as ctx:
        def sb(name, shape, dt=F32):
            return ctx.enter_context(nc.sbuf_tensor(name, shape, dt))

        def ps(name, shape, dt=F32):
            return ctx.enter_context(nc.psum_tensor(name, shape, dt))

        def sem(name):
            return ctx.enter_context(nc.semaphore(name))

        x_sb = sb("x_sb", [P, 2, TT, C])
        v_sb = sb("v_sb", [P, 2, TT, C])
        ek = sb("ek", [P, 2, TT, C])
        x1_sb = sb("x1_sb", [P, TT, C])
        state = sb("state", [P, 2, 2, T + 1])
        now = sb("now", [P, 4, 2, T])
        dn = sb("dn", [P, 4, 2, T])
        recip = sb("recip", [P, 2, 2, T])
        neg_y = sb("neg_y", [P, CC, T])
        z_sb = sb("z_sb", [P, TT, C])
        z_t = sb("z_t", [P, 2, CC, P])
        wg_sb = sb("wg_sb", [P, CC, E])
        bg_sb = sb("bg_sb", [P, E])
        td_sb = sb("td_sb", [P, CC])
        tf_sb = sb("tf_sb", [P, CC])
        decay = sb("decay", [P, CC])
        scale_a = sb("scale_a", [P, CC])
        scale_b = sb("scale_b", [P, CC])
        eps = sb("eps", [P, 1])
        bn = sb("bn", [P, 2, TT, 2, 6])
        mv = sb("mv", [P, 2, TT, 2])
        ln_tmp = sb("ln_tmp", [P, 6, 2, TT])
        rstd = sb("rstd", [P, 2, TT])
        shift = sb("shift", [P, 2, TT])

        ps_dn = ps("ps_dn", [P, 2, 2, T])
        ps_y = ps("ps_y", [P, 2, HALF])
        ps_z = ps("ps_z", [P, HALF])
        ps_lg = ps("ps_lg", [P, HALF])

        x_in = [[sem(f"x_in{par}_{t}") for t in range(TT)] for par in range(2)]
        v_in = [sem("v_in0"), sem("v_in1")]
        x1_out = sem("x1_out")
        z_out = sem("z_out")
        par_in = sem("par_in")
        eps_set = sem("eps_set")
        clipped = sem("clipped")
        dec_exp = sem("dec_exp")
        params_ready = sem("params_ready")
        ident_zero = sem("ident_zero")
        ident_ready = sem("ident_ready")
        bn_done = sem("bn_done")
        mv_ready = sem("mv_ready")
        log_done = sem("log_done")
        seed_ready = sem("seed_ready")
        refine = sem("refine")
        ln_ready = sem("ln_ready")
        ek_ready = sem("ek_ready")
        ekv_ready = sem("ekv_ready")
        first_ekv = sem("first_ekv")
        dn_t_ready = sem("dn_t_ready")
        now_ready = sem("now_ready")
        scan_done = sem("scan_done")
        dn_ready = sem("dn_ready")
        ln_den = sem("ln_den")
        recip_ready = sem("recip_ready")
        quot_ready = sem("quot_ready")
        y_ready = sem("y_ready")
        yt_ready = sem("yt_ready")
        x1_ready = sem("x1_ready")
        z_ready = sem("z_ready")
        zt_ready = sem("zt_ready")
        zt_copied = sem("zt_copied")
        lg_done = sem("lg_done")
        wide_copied = sem("wide_copied")
        router_done = sem("router_done")
        logits_out = sem("logits_out")
        waited_sp, waited_dve = sem("waited_sp"), sem("waited_dve")

        def loads(b, par):
            return b + (2 if par == 0 else 1)

        def before_start(b, back):
            return isinstance(b, int) and b < back

        def is_last(b):
            return isinstance(b, int) and b == B - 1

        def of_round(r):
            if isinstance(r, int):
                return slice(0 if r < B else 1, 1 if r < 2 else 2)
            return slice(0, 2)

        def z_buffer(b):
            return ek[:, (B - 1) % 2] if is_last(b) else z_sb[:]

        def over_batches(engine, body):
            body(0, 0)
            body(1, 1)
            with engine.Fori(2, B - 2, 2) as i:
                body(i, 0)
                body(i + 1, 1)
            body(B - 2, 0)
            body(B - 1, 1)

        block = ctx.enter_context(nc.Block())

        @block.sync
        def _(sp):
            with nc.allow_non_contiguous_dma(reason="per-channel parameters, a few KB"):
                sp.dma_start(td_sb[:], time_decay.rearrange("(c p) -> p c", p=P)).then_inc(par_in, 16)
                sp.dma_start(tf_sb[:], time_first.rearrange("(c p) -> p c", p=P)).then_inc(par_in, 16)
            sp.dma_start(wg_sb[:], w_gate.rearrange("(c p) e -> p c e", p=P)).then_inc(par_in, 16)
            sp.dma_start(bg_sb[:], b_gate.unsqueeze(0).to_broadcast([P, E])).then_inc(par_in, 16)

            def load_x(b, par):
                for t in range(TT):
                    if not before_start(b, 2):
                        sp.wait_ge(x1_ready, 2 * TT * (b - 2) + TT + t + 1)
                        sp.sem_inc(waited_sp, 1)
                    sp.dma_start(x_sb[:, par, t], x_dram[b, :, t]).then_inc(x_in[par][t], 16)

            def load_v(b, par):
                if not before_start(b, 2):
                    sp.wait_ge(dn_t_ready, CC * (b - 1))
                    sp.sem_inc(waited_sp, 1)
                sp.dma_start(v_sb[:, par], v_dram[b]).then_inc(v_in[par], 16)

            def store_x1(b):
                sp.wait_ge(x1_ready, 2 * TT * (b + 1))
                sp.dma_start(out_dram[b], x1_sb[:]).then_inc(x1_out, 16)

            def store_z(b):
                sp.wait_ge(z_ready, TT * (b + 1))
                sp.dma_start(z_out_dram[b], z_buffer(b)).then_inc(z_out, 16)

            def batch(b, par):
                if not is_last(b):
                    load_v(b + 1, 1 - par)
                    load_x(b + 1, 1 - par)
                if not before_start(b, 1):
                    store_x1(b - 1)
                    store_z(b - 1)

            load_x(0, 0)
            load_v(0, 0)
            over_batches(sp, batch)
            store_x1(B - 1)
            store_z(B - 1)
            sp.wait_ge(x1_out, 16 * B)
            sp.wait_ge(z_out, 16 * B)

        @block.gpsimd
        def _(pool):
            nc.gpsimd.memset(ident[:], 0.0).then_inc(ident_zero, 1)
            pool.wait_ge(ident_zero, 1)
            nc.gpsimd.affine_select(out=ident[:], in_=ident[:], compare_op=ALU.not_equal, fill=1.0, base=0,
                                    pattern=[[-1, P]], channel_multiplier=1).then_inc(ident_ready, 1)

            def weigh_values(b, par, t):
                pool.wait_ge(ek_ready, TT * b + t + 1)
                if t == 0:
                    pool.wait_ge(v_in[par], 8 * loads(b, par))
                nc.gpsimd.tensor_tensor(v_sb[:, par, t], ek[:, par, t], v_sb[:, par, t], ALU.mult).then_inc(ekv_ready, 1)

            def quotients(b, pair):
                r = pair % 2
                pool.wait_ge(recip_ready, PAIRS * b + pair + 1)
                nc.gpsimd.tensor_tensor(dn[:, 2 * r:2 * r + 2], dn[:, 2 * r:2 * r + 2],
                                        recip[:, r].unsqueeze(2).to_broadcast([P, 2, 2, T]),
                                        ALU.mult).then_inc(quot_ready, 1)

            def batch(b, par):
                quotients(b, 0)
                quotients(b, 1)
                if not is_last(b):
                    for t in range(TT):
                        weigh_values(b + 1, 1 - par, t)
                quotients(b, 2)
                quotients(b, 3)

            for t in range(TT // 2):
                weigh_values(0, 0, t)
            over_batches(pool, batch)

        @block.scalar
        def _(act):
            nc.scalar.add_instruction(mybir.InstLoadActFuncSet(
                act_func_set_id=EXP_LN_TABLE, name=nc.get_next_instruction_name(),
                engine=mybir.EngineType.Activation))
            act.wait_ge(par_in, 64)
            nc.scalar.activation(decay[:], td_sb[:], ACT.Exp).then_inc(dec_exp, 1)
            act.wait_ge(clipped, 2)
            nc.scalar.activation(scale_a[:], scale_a[:], ACT.Exp, scale=-1.0)
            nc.scalar.activation(scale_b[:], scale_b[:], ACT.Exp)
            act.wait_ge(dec_exp, 1)
            nc.scalar.activation(decay[:], decay[:], ACT.Exp, scale=-1.0).then_inc(params_ready, 1)
            act.wait_ge(eps_set, 1)

            def seed(r):
                which = of_round(r)
                act.wait_ge(mv_ready, r + 1)
                nc.scalar.activation(ln_tmp[:, 0, which], mv[:, which, :, 1], ACT.Ln,
                                     bias=eps[:, 0:1]).then_inc(log_done, 1)
                act.wait_ge(log_done, r + 1)
                nc.scalar.activation(ln_tmp[:, 1, which], ln_tmp[:, 0, which], ACT.Exp,
                                     scale=-0.5).then_inc(seed_ready, 1)

            def exp_k(b, par, t):
                if t == 0:
                    act.wait_ge(ln_ready, b + 1)
                nc.scalar.activation(ek[:, par, t], x_sb[:, par, t], ACT.Exp, bias=shift[:, 0, t:t + 1],
                                     scale=rstd[:, 0, t:t + 1]).then_inc(ek_ready, 1)

            def reciprocal(b, pair):
                r = pair % 2
                act.wait_ge(dn_ready, CC * b + 2 * pair + 2)
                at_least(act, y_ready, PAIRS * b + pair - 1)
                nc.scalar.activation(recip[:, r], dn[:, 2 * r:2 * r + 2, 0], ACT.Ln).then_inc(ln_den, 1)
                act.wait_ge(ln_den, PAIRS * b + pair + 1)
                nc.scalar.activation(recip[:, r], recip[:, r], ACT.Exp, scale=-1.0).then_inc(recip_ready, 1)

            def copy_z_t(b, i):
                t, h = i // 2, i % 2
                act.wait_ge(zt_ready, CC * b + i + 1)
                act.wait_ge(lg_done, TT * b + t + 1)
                nc.scalar.copy(z_t[:, t % 2, 4 * h:4 * h + 4].rearrange("p c n -> p (c n)"),
                               ps_z[:]).then_inc(zt_copied, 1)

            def scaled_now(b, c):
                act.wait_ge(dn_t_ready, CC * b + c + 1)
                at_least(act, dn_ready, CC * b + c - 3)
                nc.scalar.activation(now[:, c % 4], ps_dn[:, c % 2], ACT.Copy,
                                     scale=scale_b[:, c:c + 1]).then_inc(now_ready, 1)

            def normalise(b, t):
                if t == 0:
                    act.wait_ge(ln_ready, b + 3)
                    if not is_last(b):
                        at_least(act, z_out, 16 * b)
                        at_least(act, zt_ready, CC * b)
                nc.scalar.activation(z_buffer(b)[:, t], x1_sb[:, t], ACT.Identity, bias=shift[:, 1, t:t + 1],
                                     scale=rstd[:, 1, t:t + 1]).then_inc(z_ready, 1)

            def batch(b, par):
                has_1, has_2, last = not before_start(b, 1), not before_start(b, 2), is_last(b)

                def copy_z(i):
                    if has_2:
                        copy_z_t(b - 2, i)

                def normalise_tiles(tiles):
                    if has_1:
                        for t in tiles:
                            normalise(b - 1, t)

                def exp_tiles(tiles):
                    if not last:
                        for t in tiles:
                            exp_k(b + 1, 1 - par, t)

                scaled_now(b, 0)
                copy_z(0)
                scaled_now(b, 1)
                copy_z(1)
                scaled_now(b, 2)
                scaled_now(b, 3)
                scaled_now(b, 4)
                reciprocal(b, 0)
                copy_z(2)
                copy_z(3)
                reciprocal(b, 1)
                scaled_now(b, 5)
                copy_z(4)
                scaled_now(b, 6)
                copy_z(5)
                seed(b + 1)
                copy_z(6)
                exp_tiles((0, 1))
                copy_z(7)
                normalise_tiles((0,))
                scaled_now(b, 7)
                exp_tiles((2, 3))
                normalise_tiles((1,))
                reciprocal(b, 2)
                normalise_tiles((2, 3))
                reciprocal(b, 3)

            act.sem_inc(zt_copied, 1)
            act.wait_ge(params_ready, 1)
            seed(0)
            for t in range(TT):
                exp_k(0, 0, t)
            over_batches(act, batch)
            def copy_wide(k):
                act.wait_ge(lg_done, TT * (B - 1 + k) + 2)
                nc.scalar.copy(now[0:E, 0, k], ps_dn[0:E, 0, k]).then_inc(wide_copied, 1)

            for i in range(4):
                copy_z_t(B - 2, i)
            seed(B + 1)
            for t in range(TT):
                copy_z_t(B - 2, 4 + t)
                normalise(B - 1, t)
            for i in range(CC):
                copy_z_t(B - 1, i)
                if i == 1:
                    copy_wide(0)
            copy_wide(1)

        @block.vector
        def _(dve):
            nc.vector.memset(eps[:], LN_EPS).then_inc(eps_set, 1)
            dve.wait_ge(par_in, 64)
            nc.vector.tensor_scalar(scale_a[:], tf_sb[:], 0.0, None, ALU.max).then_inc(clipped, 1)
            nc.vector.tensor_scalar(scale_b[:], tf_sb[:], 0.0, None, ALU.min).then_inc(clipped, 1)
            BN = 2 * TT
            STEPS = 5

            def stats_of(which, src, t, h):
                return nc.vector.bn_stats(bn[:, which, t, h], src[:, t, h * HALF:(h + 1) * HALF])

            def aggregate(r, partial):
                dve.wait_ge(bn_done, partial)
                dve.sem_inc(waited_dve, 1)
                which = of_round(r)
                for w in range(which.start, which.stop):
                    for t in range(TT):
                        last = nc.vector.bn_aggr(mv[:, w, t], bn[:, w, t].rearrange("p h s -> p (h s)"))
                last.then_inc(mv_ready, 1)

            def input_stats(b, par):
                for t in range(TT):
                    dve.wait_ge(x_in[par][t], 8 * loads(b, par))
                    for h in range(2):
                        stats_of(0, x_sb[:, par], t, h).then_inc(bn_done, 1)

            def refined(r):
                which = of_round(r)
                tmp = [ln_tmp[:, k, which] for k in range(6)]
                n = STEPS * r
                dve.wait_ge(seed_ready, r + 1)
                nc.vector.tensor_tensor(tmp[2], tmp[1], tmp[1], ALU.mult).then_inc(refine, 1)
                nc.vector.tensor_scalar(tmp[3], mv[:, which, :, 1], LN_EPS, None, ALU.add).then_inc(refine, 1)
                dve.wait_ge(refine, n + 2)
                nc.vector.tensor_tensor(tmp[4], tmp[2], tmp[3], ALU.mult).then_inc(refine, 1)
                dve.wait_ge(refine, n + 3)
                nc.vector.tensor_scalar(tmp[5], tmp[4], -0.5, 1.5, ALU.mult, ALU.add).then_inc(refine, 1)
                dve.wait_ge(refine, n + 4)
                nc.vector.tensor_tensor(rstd[:, which], tmp[5], tmp[1], ALU.mult).then_inc(refine, 1)
                dve.wait_ge(refine, n + 5)
                nc.vector.scalar_tensor_tensor(shift[:, which], mv[:, which, :, 0], -1.0, rstd[:, which],
                                               ALU.mult, ALU.mult).then_inc(ln_ready, 1)

            def scan(b, c):
                n = CC * b + c
                dve.wait_ge(now_ready, n + 1)
                at_least(dve, dn_ready, n - 1)
                nc.vector.tensor_copy(state[:, c % 2, :, 0:1], ps_dn[:, c % 2, :, 0:1]).then_inc(scan_done, 1)
                for k in range(2):
                    nc.vector.tensor_tensor_scan(
                        state[:, c % 2, k, 1:T + 1], decay[:, c:c + 1].to_broadcast([P, T]), ps_dn[:, c % 2, k],
                        0.0, ALU.mult, ALU.add).then_inc(scan_done, 1)

            def combine(b, c):
                n = CC * b + c
                dve.wait_ge(scan_done, 3 * n + 3)
                if c % 2 == 0:
                    at_least(dve, y_ready, PAIRS * b + c // 2 - 1)
                nc.vector.scalar_tensor_tensor(dn[:, c % 4], state[:, c % 2, :, 0:T], scale_a[:, c:c + 1],
                                               now[:, c % 4], ALU.mult, ALU.add).then_inc(dn_ready, 1)

            def divide(b, pair):
                r = pair % 2
                dve.wait_ge(quot_ready, PAIRS * b + pair + 1)
                nc.vector.scalar_tensor_tensor(neg_y[:, 2 * pair:2 * pair + 2], dn[:, 2 * r:2 * r + 2, 0], -2.0,
                                               dn[:, 2 * r:2 * r + 2, 1], ALU.add, ALU.mult).then_inc(y_ready, 1)

            def residual(b, par, h, t):
                i = TT * h + t
                cols = slice(h * HALF, (h + 1) * HALF)
                if i == 0:
                    at_least(dve, x1_out, 16 * b)
                if h == 0:
                    at_least(dve, z_ready, TT * (b - 1) + t + 1)
                dve.wait_ge(yt_ready, 2 * TT * b + i + 1)
                nc.vector.tensor_tensor(x1_sb[:, t, cols], x_sb[:, par, t, cols], ps_y[:, i % 2],
                                        ALU.subtract).then_inc(x1_ready, 1)

            def output_stats(b, h, t):
                dve.wait_ge(x1_ready, 2 * TT * b + TT * h + t + 1)
                stats_of(1, x1_sb, t, h).then_inc(bn_done, 1)

            def second_half(b, par):
                for t in range(TT):
                    residual(b, par, 1, t)
                    if t:
                        output_stats(b, 1, t - 1)
                output_stats(b, 1, TT - 1)

            def batch(b, par):
                has_1, last = not before_start(b, 1), is_last(b)
                scan(b, 0)
                scan(b, 1)
                combine(b, 0)
                if has_1:
                    divide(b - 1, 3)
                scan(b, 2)
                combine(b, 1)
                if has_1:
                    second_half(b - 1, 1 - par)
                scan(b, 3)
                combine(b, 2)
                scan(b, 4)
                combine(b, 3)
                if not last:
                    input_stats(b + 1, 1 - par)
                aggregate(b + 1, BN * (2 * b + 2) if not last else BN * (2 * B - 1))
                scan(b, 5)
                refined(b + 1)
                divide(b, 0)
                combine(b, 4)
                scan(b, 6)
                combine(b, 5)
                divide(b, 1)
                scan(b, 7)
                combine(b, 6)
                for t in range(TT):
                    residual(b, par, 0, t)
                    if t == 1:
                        combine(b, 7)
                    if t > 1:
                        output_stats(b, 0, t - 2)
                output_stats(b, 0, TT - 2)
                output_stats(b, 0, TT - 1)
                divide(b, 2)

            input_stats(0, 0)
            aggregate(0, BN)
            refined(0)
            dve.wait_ge(v_in[0], 16)
            for t in range(TT // 2, TT):
                dve.wait_ge(ek_ready, t + 1)
                nc.vector.tensor_tensor(v_sb[:, 0, t], ek[:, 0, t], v_sb[:, 0, t], ALU.mult).then_inc(first_ekv, 1)
            dve.wait_ge(params_ready, 1)
            over_batches(dve, batch)
            divide(B - 1, 3)
            second_half(B - 1, 1)
            aggregate(B + 1, BN * 2 * B)
            refined(B + 1)
            dve.wait_ge(router_done, 2)
            nc.vector.tensor_tensor(logits[:], ps_lg[:, 0:TT * B * E].rearrange("p (n e) -> p e n", e=E),
                                    bg_sb[:].unsqueeze(2).to_broadcast([P, E, TT * B]), ALU.add).then_inc(logits_out, 1)
            dve.wait_ge(logits_out, 1)

        @block.tensor
        def _(pe):
            pe.wait_ge(ident_ready, 1)
            pe.wait_ge(par_in, 64)
            pe.sem_inc(lg_done, 2)

            def transpose_z(b, i):
                t, h = i // 2, i % 2
                pe.wait_ge(z_ready, TT * b + t + 1)
                pe.wait_ge(zt_copied, CC * b + i + 1)
                for c in range(4):
                    last = nc.tensor.transpose(ps_z[:, c * P:(c + 1) * P],
                                               z_buffer(b)[:, t, (4 * h + c) * P:(4 * h + c + 1) * P], ident[:])
                last.then_inc(zt_ready, 1)

            def route(b, t, halves=(0, 1)):
                col = E * (TT * b + t)
                for h in halves:
                    pe.wait_ge(zt_copied, CC * b + 2 * t + h + 2)
                    for c in range(4 * h, 4 * h + 4):
                        last = nc.tensor.matmul(ps_lg[:, bass.ds(col, E)], z_t[:, t % 2, c], wg_sb[:, c],
                                                start=(c == 0), stop=(c == CC - 1))
                    if h == 1:
                        last.then_inc(lg_done, 1)

            def transpose_chunk(b, par, c):
                at_least(pe, scan_done, 3 * (CC * b + c - 1))
                at_least(pe, now_ready, CC * b + c - 1)
                for k, src in enumerate((ek, v_sb)):
                    if k == 1 and c == 0:
                        pe.wait_ge(ekv_ready, TT * b + TT // 2)
                        if before_start(b, 1):
                            pe.wait_ge(first_ekv, TT // 2)
                    for t in range(TT):
                        last = nc.tensor.transpose(ps_dn[:, c % 2, k, t * P:(t + 1) * P],
                                                   src[:, par, t, c * P:(c + 1) * P], ident[:])
                last.then_inc(dn_t_ready, 1)

            def transpose_y(b, h):
                pe.wait_ge(y_ready, PAIRS * b + PAIRS // 2 * (h + 1))
                for t in range(TT):
                    i = TT * h + t
                    at_least(pe, x1_ready, 2 * TT * b + i - 1)
                    for c in range(4):
                        last = nc.tensor.transpose(ps_y[:, i % 2, c * P:(c + 1) * P],
                                                   neg_y[:, 4 * h + c, t * P:(t + 1) * P], ident[:])
                    last.then_inc(yt_ready, 1)

            def batch(b, par):
                has_1, has_2 = not before_start(b, 1), not before_start(b, 2)
                pe.wait_ge(ek_ready, TT * (b + 1))
                for c in range(CC):
                    transpose_chunk(b, par, c)
                    if has_1 and c == 3:
                        transpose_y(b - 1, 1)
                    if has_2:
                        if c == 6:
                            route(b - 2, 1)
                        for i in ((0,), (1,), (), (), (2, 3), (4,), (5, 6, 7), ())[c]:
                            transpose_z(b - 2, i)
                            if i in (2, 6):
                                route(b - 2, i // 2 - 1)
                        if c == CC - 1:
                            route(b - 2, TT - 1)
                transpose_y(b, 0)

            over_batches(pe, batch)
            def route_wide(b, t):
                k = b - (B - 2)
                pe.wait_ge(zt_copied, CC * b + 2 * t + 3)
                for c in range(CC):
                    last = nc.tensor.matmul(ps_dn[0:E, 0, k, t * P:(t + 1) * P], wg_sb[:, c], z_t[:, t % 2, c],
                                            start=(c == 0), stop=(c == CC - 1))
                last.then_inc(lg_done, 1)

            def logits_back(k):
                pe.wait_ge(wide_copied, k + 1)
                for t in range(TT):
                    col = E * (TT * (B - 2 + k) + t)
                    last = nc.tensor.transpose(ps_lg[:, col:col + E], now[0:E, 0, k, t * P:(t + 1) * P],
                                               ident[0:E, 0:E])
                last.then_inc(router_done, 1)

            transpose_z(B - 2, 0)
            transpose_z(B - 2, 1)
            pe.wait_ge(scan_done, 3 * (CC * B - 1))
            pe.wait_ge(now_ready, CC * B - 1)
            tiles = [(b, t) for b in (B - 2, B - 1) for t in range(TT)]
            for n, (b, t) in enumerate(tiles[1:]):
                transpose_z(b, 2 * t)
                route_wide(*tiles[n])
                if n == 0:
                    transpose_y(B - 1, 1)
                transpose_z(b, 2 * t + 1)
                if n == TT:
                    logits_back(0)
            route_wide(*tiles[-1])
            logits_back(1)


def feed_forward(nc, w1, w2, z_dram, out_rows, logits, ident):
    E, D, H = w1.shape
    N = z_dram.shape[0]
    NT = N // P
    CAP = N // E
    ST = CAP // P
    KD = D // P
    HALF = 512
    DH = D // HALF
    BLOCKS = 2
    GROUPS = H // (P * BLOCKS)
    NB = GROUPS * BLOCKS
    TILES = ST * DH
    BITS = 3
    DIGIT = 1 << BITS
    ROUNDS = 30 // BITS
    LIMBS = 5

    w1_v = w1.rearrange("e (k p) (g n) -> e g p k n", p=P, n=P * BLOCKS)
    w2_v = w2.rearrange("e (g b p) n -> e g p b n", p=P, b=BLOCKS)

    with ExitStack() as ctx:
        def sb(name, shape, dt=F32, stack=ctx):
            return stack.enter_context(nc.sbuf_tensor(name, shape, dt))

        def ps(name, shape, dt=F32):
            return ctx.enter_context(nc.psum_tensor(name, shape, dt))

        def sem(name):
            return ctx.enter_context(nc.semaphore(name))

        x_hi = sb("x_hi", [P, KD, CAP], F32R)
        x_lo = sb("x_lo", [P, KD, CAP], F32R)
        h_hi = sb("h_hi", [P, 2, BLOCKS, CAP], F32R)
        h_lo = sb("h_lo", [P, 2, BLOCKS, CAP], F32R)
        h_sb = sb("h_sb", [P, CAP])
        w1_hi = sb("w1_hi", [P, 2, KD, P], F32R)
        w1_lo = sb("w1_lo", [P, 2, KD, P], F32R)
        w2_hi = sb("w2_hi", [P, 2, BLOCKS, D], F32R)
        w2_lo = sb("w2_lo", [P, 2, BLOCKS, D], F32R)
        w1_raw = sb("w1_raw", [P, KD, P * BLOCKS])
        w2_raw = sb("w2_raw", [P, BLOCKS, D])
        x_raw = sb("x_raw", [P, 2, D])
        index = sb("index", [P, E, ST], U32)
        weight_now = sb("weight_now", [P, ST])
        weight = sb("weight", [P, E, ST])

        scratch = ExitStack()
        token_hot = sb("token_hot", [P, 2, NT, P], BF16, scratch)
        slot_hot = sb("slot_hot", [P, NT, ST], BF16, scratch)
        payload = sb("payload", [P, NT, LIMBS, ST], BF16, scratch)
        over = sb("over", [P, E, DIGIT - 1, NT], BF16, scratch)
        score = sb("score", [P, E, NT], F32, scratch)
        expd = sb("expd", [P, E, NT], F32, scratch)
        wins = sb("wins", [P, E, NT], F32, scratch)
        beats = sb("beats", [P, 3, 3, NT], F32, scratch)
        t0 = sb("t0", [P, E, NT], F32, scratch)
        t1 = sb("t1", [P, E, NT], F32, scratch)
        t2 = sb("t2", [P, E, NT], F32, scratch)
        t3 = sb("t3", [P, E, NT], F32, scratch)
        best = sb("best", [P, NT], F32, scratch)
        total = sb("total", [P, NT], F32, scratch)
        cand = sb("cand", [P, E, DIGIT], U32, scratch)
        digits = sb("digits", [P, DIGIT], U32, scratch)
        cut = sb("cut", [P, E], U32, scratch)
        counts = sb("counts", [P, E, DIGIT - 1], BF16, scratch)
        masks = sb("masks", [P, 2, E, NT], BF16, scratch)
        slot_u = sb("slot_u", [P, 2, E, NT], U32, scratch)
        slot_f = sb("slot_f", [P, 2, E, NT], F32, scratch)
        limbs = sb("limbs", [P, 3, E, NT], BF16, scratch)
        rest = sb("rest", [P, 2, E, NT], F32, scratch)
        iota_u = sb("iota_u", [P, P], U32, scratch)
        iota_f = sb("iota_f", [P, P], F32, scratch)
        part_u = sb("part_u", [P, 1], U32, scratch)
        ones = sb("ones", [P, P], BF16, scratch)
        before = sb("before", [P, P], BF16, scratch)
        picked = sb("picked", [P, LIMBS, ST], F32, scratch)
        tok_f = sb("tok_f", [P, 2, ST], F32, scratch)
        need = sb("need", [P, E], F32, scratch)
        scratch.close()
        acc = sb("acc", [P, ST, D])

        ps_h = ps("ps_h", [P, 2, CAP])
        ps_y = ps("ps_y2", [P, 2, HALF])
        ps_x = ps("ps_x", [P, 2, HALF])

        w1_in, w2_in = sem("w1_in"), sem("w2_in")
        w1_hi_done, w1_lo_done = sem("w1_hi_done"), sem("w1_lo_done")
        w2_hi_done, w2_lo_done = sem("w2_hi_done"), sem("w2_lo_done")
        step = sem("step")
        const_done = sem("const_done")
        score_ready = sem("score_ready")
        limb_step = sem("limb_step")
        expd_ready = sem("expd_ready")
        exp_in = sem("exp_in")
        counted = sem("counted")
        counts_ready = sem("counts_ready")
        masks_ready = sem("masks_ready")
        prefix_ready = sem("prefix_ready")
        hot_ready = sem("hot_ready")
        slots_ready = sem("slots_ready")
        index_ready = sem("index_ready")
        first_in = [sem(f"first_in{s}") for s in range(ST)]
        x_raw_in = [sem("x_raw_in0"), sem("x_raw_in1")]
        x_t_ready = sem("x_t_ready")
        x_hi_done = sem("x_hi_done")
        x_lo_done = sem("x_lo_done")
        h_mm_done = sem("h_mm_done")
        gelu_done = sem("gelu_done")
        h_hi_done, h_lo_done = sem("h_hi_done"), sem("h_lo_done")
        y_mm_done = sem("y_mm_done")
        y_added = sem("y_added")
        weight_set = sem("weight_set")
        scattered = sem("scattered")
        acc_free = sem("acc_free")

        def over_groups(engine, body):
            body(0, 0)
            body(1, 1)
            with engine.Fori(2, GROUPS - 2, 2) as i:
                body(i, 0)
                body(i + 1, 1)
            body(GROUPS - 2, 0)
            body(GROUPS - 1, 1)

        def first_rows(s):
            assert CAP == D and ST == 4 * BLOCKS
            part = (h_hi, h_lo)[s // 4]
            return part[:, s // 2 % 2, s % 2].bitcast(F32)

        def x_bank(e, s, h):
            if isinstance(e, int) and e == 0 and s % 2:
                return ps_h[:, 0, h * HALF:(h + 1) * HALF]
            return ps_x[:, h]

        def hot_operands(e):
            return (iota_f[:].unsqueeze(1).to_broadcast([P, NT, P]),
                    slot_f[:, 0, e].unsqueeze(2).to_broadcast([P, NT, P]))

        block = ctx.enter_context(nc.Block())

        @block.sync
        def _(sp):
            def load(e, g):
                done = NB * e + BLOCKS * g
                at_least(sp, w1_hi_done, done)
                at_least(sp, w1_lo_done, done)
                sp.dma_start(w1_raw[:], w1_v[e, g]).then_inc(w1_in, 16)
                at_least(sp, w2_hi_done, done)
                at_least(sp, w2_lo_done, done)
                sp.dma_start(w2_raw[:], w2_v[e, g]).then_inc(w2_in, 16)

            load(0, 0)
            with sp.Fori(1, GROUPS) as g:
                load(0, g)
            with sp.Fori(1, E) as e:
                with sp.Fori(0, GROUPS) as g:
                    load(e, g)

        @block.gpsimd
        def _(pool):
            nc.gpsimd.iota(iota_u[:], [[1, P]], base=0, channel_multiplier=0).then_inc(const_done, 1)
            nc.gpsimd.iota(part_u[:], [[1, 1]], base=0, channel_multiplier=1).then_inc(const_done, 1)
            nc.gpsimd.iota(digits[:], [[1, DIGIT]], base=0, channel_multiplier=0).then_inc(const_done, 1)
            nc.gpsimd.memset(ones[:], 1.0).then_inc(const_done, 1)
            pool.wait_ge(const_done, 4)
            nc.gpsimd.affine_select(out=before[:], in_=ones[:], compare_op=ALU.is_gt, fill=0.0, base=0,
                                    pattern=[[1, P]], channel_multiplier=-1).then_inc(const_done, 1)

            pool.wait_ge(const_done, 5)
            nc.gpsimd.tensor_copy(iota_f[:], iota_u[:])
            pool.wait_ge(score_ready, 1)
            nc.gpsimd.tensor_copy(limbs[:, 0], score[:]).then_inc(limb_step, 1)
            pool.wait_ge(limb_step, 1)
            nc.gpsimd.tensor_tensor(rest[:, 0], score[:], limbs[:, 0], ALU.subtract).then_inc(limb_step, 1)
            pool.wait_ge(limb_step, 2)
            nc.gpsimd.tensor_copy(limbs[:, 1], rest[:, 0]).then_inc(limb_step, 1)
            pool.wait_ge(limb_step, 3)
            nc.gpsimd.tensor_tensor(rest[:, 1], rest[:, 0], limbs[:, 1], ALU.subtract).then_inc(limb_step, 1)
            pool.wait_ge(limb_step, 4)
            nc.gpsimd.tensor_copy(limbs[:, 2], rest[:, 1]).then_inc(limb_step, 1)

            def gather(e, s):
                n = ST * e + s
                at_least(pool, x_t_ready, 2 * (n - 1))
                nc.gpsimd.indirect_dma_start(
                    x_raw[:, s % 2], None, z_dram,
                    bass.IndirectOffsetOnAxis(ap=index[:, e, s:s + 1], axis=0)).then_inc(x_raw_in[s % 2], 16)

            def scatter(e, s):
                pool.wait_ge(y_added, 2 + TILES * (GROUPS * e + GROUPS - 1) + DH * (s + 1))
                nc.gpsimd.indirect_dma_start(
                    out_rows, bass.IndirectOffsetOnAxis(ap=index[:, e, s:s + 1], axis=0),
                    acc[:, s], None, compute_op=ALU.add).then_inc(scattered, 16)

            pool.wait_ge(index_ready, 1)
            for s in range(ST):
                nc.gpsimd.indirect_dma_start(
                    first_rows(s), None, z_dram,
                    bass.IndirectOffsetOnAxis(ap=index[:, 0, s:s + 1], axis=0)).then_inc(first_in[s], 16)
            pool.wait_ge(index_ready, E)
            for e in range(E):
                at_least(pool, scattered, 16 * ST * e)
                pool.sem_inc(acc_free, 1)
                if e + 1 < E:
                    gather(e + 1, 0)
                    gather(e + 1, 1)
                for s in range(ST):
                    if e + 1 < E and s + 2 < ST:
                        gather(e + 1, s + 2)
                    scatter(e, s)
            pool.wait_ge(scattered, 16 * ST * E)

        @block.scalar
        def _(act):
            def split_w1(n, b):
                act.wait_ge(w1_in, 8 * (n - b) + 16)
                at_least(act, h_mm_done, n)
                nc.scalar.copy(w1_hi[:, b], w1_raw[:, :, b * P:(b + 1) * P]).then_inc(w1_hi_done, 1)

            def split_w2(n, b, par):
                act.wait_ge(w2_in, 8 * (n - b) + 16)
                nc.scalar.copy(w2_hi[:, par, b], w2_raw[:, b]).then_inc(w2_hi_done, 1)

            def split_x(e, s):
                for h in range(2):
                    act.wait_ge(x_t_ready, 2 * ST * e + 2 * s + h + 1)
                    nc.scalar.copy(x_hi[:, 4 * h:4 * h + 4, s * P:(s + 1) * P],
                                   x_bank(e, s, h).rearrange("p (k n) -> p k n", n=P)).then_inc(x_hi_done, 1)

            def expert(e):
                last_expert = isinstance(e, int) and e == E - 1

                def group(g, par):
                    for b in range(BLOCKS):
                        n = NB * e + BLOCKS * g + b
                        if not (last_expert and isinstance(g, int) and g == GROUPS - 1 and b == BLOCKS - 1):
                            split_w1(n + 1, 1 - b)
                        act.wait_ge(h_mm_done, n + 2)
                        act.wait_ge(h_lo_done, n + 1)
                        nc.scalar.activation(h_sb[:], ps_h[:, b], ACT.Gelu).then_inc(gelu_done, 1)
                        split_w2(n, b, par)
                        act.wait_ge(gelu_done, n + 1)
                        nc.scalar.copy(h_hi[:, par, b], h_sb[:]).then_inc(h_hi_done, 1)

                over_groups(act, group)

            act.wait_ge(exp_in, 1)
            nc.scalar.activation(expd[:], t0[:], ACT.Exp).then_inc(expd_ready, 1)
            split_w1(0, 0)
            for s in range(ST):
                split_x(0, s)
            def expert_and_next(e):
                expert(e)
                for s in range(ST):
                    split_x(e + 1, s)

            expert_and_next(0)
            with act.Fori(1, E - 1) as e:
                expert_and_next(e)
            expert(E - 1)

        @block.vector
        def _(dve):
            made = [0]

            def then(instruction):
                made[0] += 1
                instruction.then_inc(step, 1)
                dve.wait_ge(step, made[0])

            def tt(o, a, b, op):
                return nc.vector.tensor_tensor(o, a, b, op)

            dve.wait_ge(const_done, 5)
            for e in range(E - 1):
                last = tt(beats[:, e, e:], logits[:, e:e + 1].to_broadcast([P, E - 1 - e, NT]), logits[:, e + 1:],
                          ALU.is_ge)
            then(last)
            then(tt(t1[:, 0:2], logits[:, 0:2], logits[:, 2:4], ALU.max))
            then(tt(best[:], t1[:, 0], t1[:, 1], ALU.max))
            then(tt(t0[:], logits[:], best[:].unsqueeze(1).to_broadcast([P, E, NT]), ALU.subtract))
            nc.vector.engine_nop().then_inc(exp_in, 1)
            g = lambda e, f: beats[:, e, f - 1]
            then(tt(t1[:, 0], g(0, 1), g(0, 2), ALU.add))
            then(tt(wins[:, 0], t1[:, 0], g(0, 3), ALU.add))
            then(tt(t1[:, 1], g(1, 2), g(1, 3), ALU.add))
            then(tt(t2[:, 1], t1[:, 1], g(0, 1), ALU.subtract))
            then(nc.vector.tensor_scalar(wins[:, 1], t2[:, 1], 1.0, None, ALU.add))
            then(tt(t1[:, 2], g(2, 3), g(0, 2), ALU.subtract))
            then(tt(t2[:, 2], t1[:, 2], g(1, 2), ALU.subtract))
            then(nc.vector.tensor_scalar(wins[:, 2], t2[:, 2], 2.0, None, ALU.add))
            then(tt(t1[:, 3], g(0, 3), g(1, 3), ALU.add))
            then(tt(t2[:, 3], t1[:, 3], g(2, 3), ALU.add))
            then(nc.vector.tensor_scalar(wins[:, 3], t2[:, 3], -1.0, 3.0, ALU.mult, ALU.add))
            dve.wait_ge(expd_ready, 1)
            then(nc.vector.scalar_tensor_tensor(t1[:], wins[:], float(E - TOPK), expd[:], ALU.is_ge, ALU.mult))
            then(tt(t2[:, 0:2], t1[:, 0:2], t1[:, 2:4], ALU.add))
            then(tt(total[:], t2[:, 0], t2[:, 1], ALU.add))
            then(nc.vector.reciprocal(best[:], total[:]))
            then(tt(score[:], t1[:], best[:].unsqueeze(1).to_broadcast([P, E, NT]), ALU.mult))
            nc.vector.engine_nop().then_inc(score_ready, 1)
            then(nc.vector.memset(cut[:], 0))
            then(nc.vector.tensor_scalar(digits[:], digits[:], BITS * (ROUNDS - 1), None, ALU.logical_shift_left))
            SEARCH = 5
            base = made[0]
            cut_f, cand_f = cut[:].bitcast(F32), cand[:].bitcast(F32)
            with dve.Fori(0, ROUNDS) as i:
                done = base + SEARCH * i
                dve.wait_ge(step, done)
                tt(cand[:], cut[:].unsqueeze(2).to_broadcast([P, E, DIGIT]),
                   digits[:].unsqueeze(1).to_broadcast([P, E, DIGIT]), ALU.bitwise_or).then_inc(step, 1)
                dve.wait_ge(step, done + 1)
                tt(over[:], score[:].unsqueeze(2).to_broadcast([P, E, DIGIT - 1, NT]),
                   cand_f[:, :, 1:].unsqueeze(3).to_broadcast([P, E, DIGIT - 1, NT]), ALU.is_ge).then_inc(step, 1)
                dve.wait_ge(step, done + 2)
                with nc.allow_low_precision(reason="counts up to 32 are exact in bfloat16"):
                    nc.vector.tensor_reduce(counts[:], over[:], AX_X, ALU.add).then_inc(counts_ready, 1)
                nc.vector.tensor_scalar(digits[:], digits[:], BITS, None, ALU.logical_shift_right).then_inc(step, 1)
                dve.wait_ge(step, done + 3)
                dve.wait_ge(counted, i + 1)
                nc.vector.scalar_tensor_tensor(
                    cand_f[:, :, 1:], ps_x[:, 0, 0:E * (DIGIT - 1)].rearrange("p (e d) -> p e d", e=E),
                    float(CAP) - 0.5, cand_f[:, :, 1:], ALU.is_ge, ALU.mult).then_inc(step, 1)
                dve.wait_ge(step, done + 4)
                nc.vector.tensor_reduce(cut_f, cand_f, AX_X, ALU.max).then_inc(step, 1)
            made[0] = base + SEARCH * ROUNDS
            dve.wait_ge(step, made[0])
            cut_b = cut_f.unsqueeze(2).to_broadcast([P, E, NT])
            tt(masks[:, 0], score[:], cut_b, ALU.is_gt)
            then(tt(masks[:, 1], score[:], cut_b, ALU.is_equal))
            nc.vector.engine_nop().then_inc(masks_ready, 1)

            EN = E * NT
            dve.wait_ge(prefix_ready, 1)
            within = ps_h[:, 0, 0:2 * EN].rearrange("p (m e n) -> p m e n", m=2, e=E)
            totals = ps_h[:, 1, 0:2 * EN].rearrange("p (m e n) -> p m e n", m=2, e=E)
            for m, t in ((0, t0), (1, t1)):
                for e in range(E):
                    last = nc.vector.tensor_tensor_scan(t[:, e], ones[:, 0:1].to_broadcast([P, NT]),
                                                        totals[:, m, e], 0.0, ALU.mult, ALU.add)
            then(last)
            then(nc.vector.tensor_scalar(need[:], t0[:, :, NT - 1], -1.0, float(CAP), ALU.mult, ALU.add))
            then(tt(t2[:], t0[:], totals[:, 0], ALU.subtract))
            then(tt(t3[:], t2[:], within[:, 0], ALU.add))
            then(tt(t2[:], t1[:], totals[:, 1], ALU.subtract))
            then(tt(t0[:], t2[:], within[:, 1], ALU.add))
            need_b = need[:].unsqueeze(2).to_broadcast([P, E, NT])
            then(tt(t1[:], t0[:], need_b, ALU.is_lt))
            then(tt(t2[:], t1[:], masks[:, 1], ALU.mult))
            then(tt(wins[:], t2[:], masks[:, 0], ALU.add))
            then(tt(t1[:], t0[:], need_b, ALU.min))
            then(tt(t2[:], t3[:], t1[:], ALU.add))
            then(nc.vector.tensor_scalar(t1[:], wins[:], float(-N), float(N), ALU.mult, ALU.add))
            then(tt(slot_u[:, 0], t2[:], t1[:], ALU.add))
            then(nc.vector.tensor_scalar(slot_u[:, 1], slot_u[:, 0], P.bit_length() - 1, None,
                                         ALU.logical_shift_right))
            then(nc.vector.tensor_scalar(slot_u[:, 0], slot_u[:, 0], P - 1, None, ALU.bitwise_and))
            then(nc.vector.tensor_copy(slot_f[:], slot_u[:]))
            def one_hot(e):
                at_least(dve, slots_ready, e - 1)
                if e == 0:
                    dve.wait_ge(limb_step, 5)
                then(tt(token_hot[:, e % 2], *hot_operands(e), ALU.is_equal))

            def payloads(e):
                at_least(dve, slots_ready, e)
                then(tt(slot_hot[:], iota_f[:, 0:ST].unsqueeze(1).to_broadcast([P, NT, ST]),
                        slot_f[:, 1, e].unsqueeze(2).to_broadcast([P, NT, ST]), ALU.is_equal))
                tt(payload[:, :, 0], slot_hot[:], iota_f[:, 0:NT].unsqueeze(2).to_broadcast([P, NT, ST]), ALU.mult)
                tt(payload[:, :, 1], slot_hot[:], part_u[:].unsqueeze(2).to_broadcast([P, NT, ST]), ALU.mult)
                for k in range(3):
                    last = tt(payload[:, :, 2 + k], slot_hot[:],
                              limbs[:, k, e].unsqueeze(2).to_broadcast([P, NT, ST]), ALU.mult)
                last.then_inc(hot_ready, 1)

            def read_lists(e):
                dve.wait_ge(slots_ready, e + 1)
                then(nc.vector.tensor_copy(picked[:].rearrange("p l s -> p (l s)"), ps_y[:, e % 2, 0:LIMBS * ST]))
                nc.vector.tensor_scalar(tok_f[:, 0], picked[:, 0], float(P), None, ALU.mult)
                then(tt(tok_f[:, 1], picked[:, 2], picked[:, 3], ALU.add))
                then(tt(index[:, e], tok_f[:, 0], picked[:, 1], ALU.add))
                nc.vector.engine_nop().then_inc(index_ready, 1)
                then(tt(weight[:, e], tok_f[:, 1], picked[:, 4], ALU.add))

            def split_w1(n, b):
                dve.wait_ge(w1_hi_done, n + 1)
                tt(w1_lo[:, b], w1_raw[:, :, b * P:(b + 1) * P], w1_hi[:, b].bitcast(F32),
                   ALU.subtract).then_inc(w1_lo_done, 1)

            def split_w2(n, b, par, half):
                cols = slice(half * HALF, (half + 1) * HALF)
                if half == 0:
                    dve.wait_ge(w2_hi_done, n + 1)
                low = tt(w2_lo[:, par, b, cols], w2_raw[:, b, cols], w2_hi[:, par, b, cols].bitcast(F32), ALU.subtract)
                if half == 1:
                    low.then_inc(w2_lo_done, 1)

            def split_h(n, b, par, half):
                cols = slice(half * HALF, (half + 1) * HALF)
                if half == 0:
                    dve.wait_ge(h_hi_done, n + 1)
                low = tt(h_lo[:, par, b, cols], h_sb[:, cols], h_hi[:, par, b, cols].bitcast(F32), ALU.subtract)
                if half == 1:
                    low.then_inc(h_lo_done, 1)

            def split_x(e, s):
                for h in range(2):
                    dve.wait_ge(x_hi_done, 2 * ST * e + 2 * s + h + 1)
                    cols = slice(s * P, (s + 1) * P)
                    tt(x_lo[:, 4 * h:4 * h + 4, cols], x_bank(e, s, h).rearrange("p (k n) -> p k n", n=P),
                       x_hi[:, 4 * h:4 * h + 4, cols].bitcast(F32), ALU.subtract).then_inc(x_lo_done, 1)

            def add_y(e, g, tile):
                s, dh = tile // DH, tile % DH
                a = acc[:, s, dh * HALF:(dh + 1) * HALF]
                if isinstance(g, int) and g == 0:
                    if tile == 0:
                        dve.wait_ge(acc_free, e + 1)
                    dve.wait_ge(y_mm_done, TILES * (GROUPS * e + g) + tile + 1)
                    nc.vector.tensor_scalar(a, ps_y[:, tile % 2], weight_now[:, s:s + 1], None,
                                            ALU.mult).then_inc(y_added, 1)
                    return
                dve.wait_ge(y_mm_done, TILES * (GROUPS * e + g) + tile + 1)
                nc.vector.scalar_tensor_tensor(a, ps_y[:, tile % 2], weight_now[:, s:s + 1], a, ALU.mult,
                                               ALU.add).then_inc(y_added, 1)

            def expert(e):
                last_expert = isinstance(e, int) and e == E - 1

                def group(g, par):
                    first = isinstance(g, int) and g == 0
                    for b in range(BLOCKS):
                        n = NB * e + BLOCKS * g + b
                        if not (last_expert and isinstance(g, int) and g == GROUPS - 1 and b == BLOCKS - 1):
                            split_w1(n + 1, 1 - b)
                        start = first and isinstance(e, int) and e == 0
                        if start and b == 0:
                            one_hot(2)
                            payloads(2)
                            one_hot(3)
                        tiles = [] if first else list(range(b * TILES // 2, (b + 1) * TILES // 2))
                        splits = [(split_h, 0), (split_h, 1), (split_w2, 0), (split_w2, 1)]
                        for at, tile in enumerate(tiles):
                            add_y(e, g - 1, tile)
                            if 1 <= at <= len(splits):
                                split, half = splits[at - 1]
                                split(n, b, par, half)
                        if not tiles:
                            for split, half in splits:
                                split(n, b, par, half)
                        if start:
                            read_lists(2 + b)
                            if b == 0:
                                payloads(3)
                            else:
                                dve.sem_inc(y_added, 2)

                over_groups(dve, group)

            dve.sem_inc(h_lo_done, 1)
            one_hot(0)
            payloads(0)
            read_lists(0)
            one_hot(1)
            split_w1(0, 0)
            split_x(0, 0)
            payloads(1)
            split_x(0, 1)
            read_lists(1)
            for s in range(2, ST):
                split_x(0, s)

            def take_weights(e):
                if not (isinstance(e, int) and e == 0):
                    dve.wait_ge(y_added, 2 + TILES * GROUPS * e)
                nc.vector.tensor_copy(weight_now[:], weight[:, e]).then_inc(weight_set, 1)
                dve.wait_ge(weight_set, e + 1)

            def expert_and_next(e):
                take_weights(e)
                expert(e)
                for s in range(ST):
                    split_x(e + 1, s)
                    for dh in range(DH):
                        add_y(e, GROUPS - 1, DH * s + dh)

            expert_and_next(0)
            with dve.Fori(1, E - 1) as e:
                expert_and_next(e)
            take_weights(E - 1)
            expert(E - 1)
            for tile in range(TILES):
                add_y(E - 1, GROUPS - 1, tile)

        @block.tensor
        def _(pe):
            pe.wait_ge(const_done, 5)
            with pe.Fori(0, ROUNDS) as i:
                pe.wait_ge(counts_ready, i + 1)
                nc.tensor.matmul(ps_x[:, 0, 0:E * (DIGIT - 1)], ones[:], counts[:].rearrange("p e d -> p (e d)"),
                                 start=True, stop=True).then_inc(counted, 1)
            pe.wait_ge(masks_ready, 1)
            flat = masks[:].rearrange("p m e n -> p (m e n)")
            nc.tensor.matmul(ps_h[:, 0, 0:2 * E * NT], before[:], flat, start=True, stop=True)
            nc.tensor.matmul(ps_h[:, 1, 0:2 * E * NT], ones[:], flat, start=True, stop=True).then_inc(prefix_ready, 1)

            def lists(e):
                pe.wait_ge(hot_ready, e + 1)
                at_least(pe, index_ready, e - 1)
                for j in range(NT):
                    last = nc.tensor.matmul(ps_y[:, e % 2, 0:LIMBS * ST], token_hot[:, e % 2, j],
                                            payload[:, j].rearrange("p l s -> p (l s)"),
                                            start=(j == 0), stop=(j == NT - 1))
                last.then_inc(slots_ready, 1)

            def transpose_x(e, s):
                first = isinstance(e, int) and e == 0
                rows = first_rows(s) if first else x_raw[:, s % 2]
                if first:
                    pe.wait_ge(first_in[s], 16)
                else:
                    pe.wait_ge(x_raw_in[s % 2], 16 * (ST // 2) * (e - 1) + 16 * (s // 2 + 1))
                for h in range(2):
                    bank = x_bank(e, s, h)
                    at_least(pe, x_lo_done, 2 * ST * e + 2 * (s - 2 if first else s - 1) + h + 1)
                    for k in range(4):
                        last = nc.tensor.transpose(bank[:, k * P:(k + 1) * P],
                                                   rows[:, (4 * h + k) * P:(4 * h + k + 1) * P], ident[:])
                    last.then_inc(x_t_ready, 1)

            def product(out, hi_lo_l, hi_lo_r, k, count, first, stop):
                (lh, ll), (rh, rl) = hi_lo_l, hi_lo_r
                nc.tensor.matmul(out, lh, rh, start=first, stop=False)
                nc.tensor.matmul(out, lh, rl, start=False, stop=False)
                return nc.tensor.matmul(out, ll, rh, start=False, stop=stop)

            def hidden(e, g, b):
                n = NB * e + BLOCKS * g + b
                pe.wait_ge(w1_hi_done, n + 1)
                pe.wait_ge(w1_lo_done, n + 1)
                for half in range(2):
                    cols = slice(half * HALF, (half + 1) * HALF)
                    for k in range(KD):
                        last = product(ps_h[:, b, cols], (w1_hi[:, b, k], w1_lo[:, b, k]),
                                       (x_hi[:, k, cols], x_lo[:, k, cols]), k, KD, k == 0, k == KD - 1)
                last.then_inc(h_mm_done, 1)

            def outputs(e, g, par, tile):
                n = GROUPS * e + g
                s, dh = tile // DH, tile % DH
                if tile == 0:
                    for done in (h_hi_done, w2_hi_done, w2_lo_done):
                        pe.wait_ge(done, BLOCKS * (n + 1))
                    pe.wait_ge(h_lo_done, BLOCKS * (n + 1) + 1)
                pe.wait_ge(y_added, TILES * n + tile + 1)
                rows, cols = slice(s * P, (s + 1) * P), slice(dh * HALF, (dh + 1) * HALF)
                for b in range(BLOCKS):
                    last = product(ps_y[:, tile % 2], (h_hi[:, par, b, rows], h_lo[:, par, b, rows]),
                                   (w2_hi[:, par, b, cols], w2_lo[:, par, b, cols]), b, BLOCKS, b == 0,
                                   b == BLOCKS - 1)
                last.then_inc(y_mm_done, 1)

            def expert(e):
                pe.wait_ge(x_lo_done, 2 * ST * (e + 1))

                def group(g, par):
                    for b in range(BLOCKS):
                        hidden(e, g, b)
                        if isinstance(g, int) and g == 0 and isinstance(e, int) and e == 0:
                            lists(2 + b)
                        if not (isinstance(g, int) and g == 0):
                            for tile in range(b * TILES // 2, (b + 1) * TILES // 2):
                                outputs(e, g - 1, 1 - par, tile)

                over_groups(pe, group)

            pe.sem_inc(h_mm_done, 1)
            lists(0)
            for s in range(ST):
                transpose_x(0, s)
                if s == 1:
                    lists(1)

            def expert_and_next(e):
                expert(e)
                for s in range(ST):
                    transpose_x(e + 1, s)
                    for dh in range(DH):
                        outputs(e, GROUPS - 1, (GROUPS - 1) % 2, DH * s + dh)

            expert_and_next(0)
            with pe.Fori(1, E - 1) as e:
                expert_and_next(e)
            expert(E - 1)
            for tile in range(TILES):
                outputs(E - 1, GROUPS - 1, (GROUPS - 1) % 2, tile)


def build(nc, x, ctx_2048, L0_xattn_time_decay, L0_xattn_time_first, L0_ffn_Wg, L0_ffn_bg, L0_ffn_W1, L0_ffn_W2, out):
    B, T, C = x.shape
    E = L0_ffn_Wg.shape[1]
    z_dram = nc.dram_tensor("z_rows", (B * T, C), F32, kind="Internal").ap()
    with nc.sbuf_tensor("logits", [P, E, B * T // P], F32) as logits, nc.sbuf_tensor("ident", [P, P], F32) as ident:
        token_mixing(nc, x, ctx_2048, L0_xattn_time_decay, L0_xattn_time_first, L0_ffn_Wg, L0_ffn_bg, out, z_dram,
                     logits, ident)
        feed_forward(nc, L0_ffn_W1, L0_ffn_W2, z_dram, out.rearrange("b t c -> (b t) c"), logits, ident)


_INS = ['x', 'ctx_2048', 'L0_xattn_time_decay', 'L0_xattn_time_first', 'L0_ffn_Wg', 'L0_ffn_bg', 'L0_ffn_W1',
        'L0_ffn_W2']


def kernel(**inputs):
    import numpy as _np
    import concourse.bacc as _bacc
    from concourse import mybir as _mybir
    from concourse.bass_utils import run_bass_kernel_spmd as _run

    nc = _bacc.Bacc("TRN2", target_bir_lowering=False, num_devices=1)
    arrays, args = {}, []
    for name in _INS:
        a = _np.ascontiguousarray(inputs[name])
        arrays[f"in_{name}_dram"] = a
        args.append(nc.dram_tensor(f"in_{name}_dram", a.shape, _mybir.dt.from_np(a.dtype), kind="ExternalInput").ap())
    out = nc.dram_tensor("out_0_dram", inputs["x"].shape, _mybir.dt.float32, kind="ExternalOutput").ap()
    build(nc, *args, out)
    r = _run(nc, [arrays], core_ids=[0])
    return r.results[0]["out_0_dram"]
```
